# Optimizing a Trainium2 kernel written in Bass

```python
import numpy as np
import jax
import jax.numpy as jnp

def _softmax(x, axis=-1):
    return jax.nn.softmax(x, axis=axis)

def _gelu(x):
    return jax.nn.gelu(x, approximate=True)

def _silu(x):
    return jax.nn.silu(x)

def _sigmoid(x):
    return jax.nn.sigmoid(x)

def _layernorm(x, axis=-1, eps=1e-05):
    m = jnp.mean(x, axis=axis, keepdims=True)
    v = jnp.var(x, axis=axis, keepdims=True)
    return (x - m) / jnp.sqrt(v + eps)

def _scatter_add(tgt, idx, src, axis=0):
    return tgt.at[idx].add(src)

def _segment_sum(src, seg, n):
    return jax.ops.segment_sum(src, seg, n)
kernel_name = 'mk_prb_d1_jaxref_r4_fb2474'

def setup_inputs(seed: int=0):
    np.random.seed(seed)
    _w = jnp.asarray

    def _L0_attn_setup():
        import jax, jax.numpy as jnp
        import numpy as np
        B, S, E = (2, 512, 256)
        H, D = (16, 64)

        def _attention(q, k, v):
            dtype = q.dtype
            logits = jnp.einsum('bqhd,bkhd->bhqk', q.astype(jnp.float32), k.astype(jnp.float32))
            logits = logits / jnp.sqrt(jnp.float32(q.shape[-1]))
            mask = jnp.tril(jnp.ones((q.shape[1], q.shape[1]), dtype=jnp.bool_))
            neg = jnp.asarray(-0.7 * jnp.finfo(logits.dtype).max, dtype=logits.dtype)
            logits = jnp.where(mask, logits, neg)
            probs = jax.nn.softmax(logits, axis=-1).astype(dtype)
            return jnp.einsum('bhqk,bkhd->bqhd', probs, v)
        key = jax.random.key(seed)
        k1, k2, k3 = jax.random.split(key, 3)
        x = jax.random.normal(k1, (B, S, E), dtype=jnp.float32)
        w_qkv = jax.random.normal(k2, (E, H, 3 * D), dtype=jnp.float32) * 0.01
        w_out = jax.random.normal(k3, (H, D, E), dtype=jnp.float32) * 0.01
        return {'x': x, 'w_qkv': w_qkv, 'w_out': w_out}
    _L0_attn_in = _L0_attn_setup()

    def _L0_ffn_setup():
        import jax, jax.numpy as jnp
        import numpy as np
        E = 8
        K = 2
        CAP_FACTOR = 1.0
        key = jax.random.key(seed)
        k0, k1, k2, k3 = jax.random.split(key, 4)
        B, S, M, H = (4, 512, 256, 1024)
        x = jax.random.normal(k0, (B, S, M), jnp.float32)
        wg = jax.random.normal(k1, (M, E), jnp.float32) * 0.02
        w1 = jax.random.normal(k2, (E, M, H), jnp.float32) * 0.02
        b1 = jnp.zeros((E, H), jnp.float32)
        w2 = jax.random.normal(k3, (E, H, M), jnp.float32) * 0.02
        b2 = jnp.zeros((E, M), jnp.float32)
        return {'x': x, 'wg': wg, 'w1': w1, 'b1': b1, 'w2': w2, 'b2': b2}
    _L0_ffn_in = _L0_ffn_setup()
    _d = {'L0_attn_x': _L0_attn_in['x'], 'L0_attn_w_qkv': _L0_attn_in['w_qkv'], 'L0_attn_w_out': _L0_attn_in['w_out'], 'L0_ffn_wg': _L0_ffn_in['wg'], 'L0_ffn_w1': _L0_ffn_in['w1'], 'L0_ffn_b1': _L0_ffn_in['b1'], 'L0_ffn_w2': _L0_ffn_in['w2'], 'L0_ffn_b2': _L0_ffn_in['b2']}
    _x0 = _d['L0_attn_x']
    _d['L0_attn_x'] = jax.random.normal(jax.random.fold_in(jax.random.key(seed), 1), (8, 1024, 256), dtype=_x0.dtype)
    del _x0
    return _d

def reference(L0_attn_x, L0_attn_w_qkv, L0_attn_w_out, L0_ffn_wg, L0_ffn_w1, L0_ffn_b1, L0_ffn_w2, L0_ffn_b2):

    def _L0_attn_ref(x, w_qkv, w_out):
        import jax, jax.numpy as jnp
        import numpy as np
        B, S, E = (2, 512, 256)
        H, D = (16, 64)

        def _attention(q, k, v):
            dtype = q.dtype
            logits = jnp.einsum('bqhd,bkhd->bhqk', q.astype(jnp.float32), k.astype(jnp.float32))
            logits = logits / jnp.sqrt(jnp.float32(q.shape[-1]))
            mask = jnp.tril(jnp.ones((q.shape[1], q.shape[1]), dtype=jnp.bool_))
            neg = jnp.asarray(-0.7 * jnp.finfo(logits.dtype).max, dtype=logits.dtype)
            logits = jnp.where(mask, logits, neg)
            probs = jax.nn.softmax(logits, axis=-1).astype(dtype)
            return jnp.einsum('bhqk,bkhd->bqhd', probs, v)
        qkv = jnp.einsum('bse,ehd->bshd', x, w_qkv)
        q, k, v = jnp.split(qkv, 3, axis=-1)
        out = _attention(q, k, v)
        return jnp.einsum('bshd,hde->bse', out, w_out)

    def _L0_ffn_ref(x, wg, w1, b1, w2, b2):
        import jax, jax.numpy as jnp
        import numpy as np
        E = 8
        K = 2
        CAP_FACTOR = 1.0
        B, S, M = x.shape
        N = B * S
        capacity = int(CAP_FACTOR * K * N // E)
        xt = x.reshape(N, M)
        logits = xt @ wg
        scores = jax.nn.softmax(logits, axis=-1)
        topv, topi = jax.lax.top_k(scores, K)
        topv = topv / jnp.sum(topv, axis=-1, keepdims=True)
        masks = jax.nn.one_hot(topi.T, E, dtype=jnp.int32)
        flat = masks.reshape(K * N, E)
        locs = jnp.cumsum(flat, axis=0) - 1
        pos = jnp.sum(locs * flat, axis=-1).reshape(K, N).T
        valid = pos < capacity
        gate = topv * valid.astype(topv.dtype)
        pos_c = jnp.where(valid, pos, 0)
        xk = xt[:, None, :] * valid[..., None].astype(xt.dtype)
        disp = jnp.zeros((E, capacity, M), xt.dtype)
        disp = disp.at[topi, pos_c].add(xk)
        h = jax.nn.relu(jnp.einsum('ecm,emh->ech', disp, w1) + b1[:, None, :])
        y = jnp.einsum('ech,ehm->ecm', h, w2) + b2[:, None, :]
        out = jnp.sum(gate[..., None] * y[topi, pos_c], axis=1)
        return out.reshape(B, S, M)
    x = L0_attn_x
    xn = _layernorm(x, axis=-1)
    x = x + _L0_attn_ref(xn, L0_attn_w_qkv, L0_attn_w_out) + _L0_ffn_ref(xn, L0_ffn_wg, L0_ffn_w1, L0_ffn_b1, L0_ffn_w2, L0_ffn_b2)
    return x

_drawn_inputs = setup_inputs


def setup_inputs(seed=0):
    import zlib

    import numpy as np

    out = dict(_drawn_inputs(seed))
    spreads = {'L0_ffn_b1': (0.0, 0.308), 'L0_ffn_b2': (0.0, 0.1)}
    factors = {'L0_attn_w_qkv': 8.0, 'L0_attn_w_out': 8.0}
    for name, (base, spread) in spreads.items():
        noise = np.random.default_rng([zlib.crc32(name.encode()), seed]).standard_normal(out[name].shape)
        drawn = base * np.exp(spread * noise) if base else spread * noise
        out[name] = jnp.asarray(drawn.astype(out[name].dtype))
    for name, factor in factors.items():
        out[name] = (out[name] * factor).astype(out[name].dtype)
    return out
```

```python
from contextlib import ExitStack

import numpy as np

import concourse.bass as bass
from concourse import mybir

F32, F32R, BF16 = mybir.dt.float32, mybir.dt.float32r, mybir.dt.bfloat16
U32 = mybir.dt.uint32
ALU, ACT, AX = mybir.AluOpType, mybir.ActivationFunctionType, mybir.AxisListType

P = 128
BATCH, SEQ, MODEL = 8, 1024, 256
TOKENS = BATCH * SEQ
TILES = TOKENS // P
MC = MODEL // P
HEADS, HDIM = 16, 64
PAIRS = HEADS // 2
QT = SEQ // P
EXPERTS, TOPK, HIDDEN = 8, 2, 1024
CAP = TOPK * TOKENS // EXPERTS
SLOTS = EXPERTS * CAP
HC = HIDDEN // P
EPS = 1e-5
QSCALE = HDIM ** -0.5
MASKED = -0.7 * 3.3895314e38


class Count:

    def __init__(self, sem, per):
        self.sem, self.per = sem, per

    def wait(self, eng, n, k):
        eng.wait_ge(self.sem, n * self.per + k)


def apart(eng, sem):
    eng.sem_inc(sem, 1)


def constants(nc, ctx):
    t = {}
    for name, dt in (("ident", F32), ("identb", BF16), ("mask", BF16), ("upper", BF16), ("ones", BF16)):
        t[name] = ctx.enter_context(nc.sbuf_tensor(name, [P, P], dt))
    with ExitStack() as tmp:
        s_set, s_done = (tmp.enter_context(nc.semaphore(n)) for n in ("s_const_set", "s_const"))
        block = tmp.enter_context(nc.Block())

        @block.gpsimd
        def _(g):
            g.memset(t["ident"][:], 0.0)
            g.memset(t["identb"][:], 0.0)
            g.memset(t["mask"][:], 0.0)
            g.memset(t["ones"][:], 1.0)
            g.memset(t["upper"][:], 1.0).then_inc(s_set, 1)
            g.wait_ge(s_set, 1)
            for name in ("ident", "identb"):
                g.affine_select(t[name][:], t[name][:], [[-1, P]], ALU.not_equal, 1.0, base=0, channel_multiplier=1)
            g.affine_select(t["mask"][:], t["mask"][:], [[-1, P]], ALU.is_ge, MASKED, base=0, channel_multiplier=1)
            g.affine_select(t["upper"][:], t["upper"][:], [[1, P]], ALU.is_gt, 0.0, base=0,
                            channel_multiplier=-1).then_inc(s_done, 1)
            g.wait_ge(s_done, 1)
    return t


def layernorm_and_router(nc, k, x, wg, xn_dram, logits):
    UT = 4
    UNITS = TILES // UT
    xv = x.rearrange("b s m -> (b s) m").rearrange("(u t p) m -> u p t m", t=UT, p=P)
    xnv = xn_dram.rearrange("(u t p) m -> u p t m", t=UT, p=P)
    with ExitStack() as c:
        sb = lambda n, s, d=F32: c.enter_context(nc.sbuf_tensor(n, s, d))
        ps = lambda n, s: c.enter_context(nc.psum_tensor(n, s, F32))
        sem = lambda n: c.enter_context(nc.semaphore(n))
        x4 = [sb(f"x4_{i}", [P, UT, MODEL]) for i in range(2)]
        xn4 = [sb(f"xn4_{i}", [P, UT, MODEL]) for i in range(2)]
        xT = [sb(f"xT_{i}", [P, UT * MC, P]) for i in range(2)]
        stats = [sb(f"stats_{i}", [P, UT, 6]) for i in range(2)]
        mv = [sb(f"mv_{i}", [P, UT, 2]) for i in range(2)]
        std = [sb(f"std_{i}", [P, UT]) for i in range(2)]
        rstd = [sb(f"rstd_{i}", [P, UT]) for i in range(2)]
        wg_sb = sb("wg_sb", [P, MC, EXPERTS])
        eps = sb("eps", [P, 1])
        pT = [ps(f"pT_{i}", [P, 2, 512]) for i in range(2)]
        pL = [ps(f"pL_{i}", [P, UT, EXPERTS]) for i in range(2)]
        in_ = [Count(sem(f"s_in{i}"), 16) for i in range(2)]
        out_ = [Count(sem(f"s_out{i}"), 16) for i in range(2)]
        s_wg, s_eps, s_apart = sem("s_wg"), sem("s_eps"), sem("s_apart_ln")
        stat = Count(sem("s_stat"), 1)
        aggr = Count(sem("s_aggr"), 1)
        root = Count(sem("s_root"), 1)
        rec = Count(sem("s_rec"), 1)
        norm = Count(sem("s_norm"), 1)
        tr = Count(sem("s_tr"), 1)
        trc = Count(sem("s_trc"), 1)
        lg = Count(sem("s_lg"), 1)
        lgc = Count(sem("s_lgc"), 1)
        block = c.enter_context(nc.Block())
        HALF = UNITS // 2

        @block.sync
        def _(e):
            e.dma_start(wg_sb[:], wg.rearrange("(c p) n -> p c n", p=P)).then_inc(s_wg, 16)
            for q in range(2):
                e.dma_start(x4[q][:], xv[q]).then_inc(in_[q].sem, 16)
            with e.Fori(0, HALF - 1) as i:
                for q in range(2):
                    u = i * 2 + q
                    norm.wait(e, u, 1)
                    e.dma_start(x4[q][:], xv[bass.ds(u + 2, 1)].rearrange("u p t m -> (u p) t m")).then_inc(in_[q].sem, 16)
                    e.dma_start(xnv[bass.ds(u, 1)].rearrange("u p t m -> (u p) t m"), xn4[q][:]).then_inc(out_[q].sem, 16)
            for q in range(2):
                u = UNITS - 2 + q
                norm.wait(e, u, 1)
                e.dma_start(xnv[u], xn4[q][:]).then_inc(out_[q].sem, 16)
            for q in range(2):
                out_[q].wait(e, HALF - 1, 16)

        @block.scalar
        def _(e):
            e.wait_ge(s_eps, 1)
            with e.Fori(0, HALF) as i:
                for q in range(2):
                    u = i * 2 + q
                    aggr.wait(e, u, 1)
                    e.activation(std[q][:], mv[q][:, :, 1], ACT.Sqrt, bias=eps[:, 0:1]).then_inc(root.sem, 1)
                    tr.wait(e, u, 1)
                    for h in range(2):
                        ins = e.activation(xT[q][:, 4 * h:4 * h + 4, :].rearrange("p a b -> p (a b)"), pT[q][:, h, :], ACT.Copy)
                    ins.then_inc(trc.sem, 1)

        @block.vector
        def _(e):
            e.memset(eps[:], EPS).then_inc(s_eps, 1)

            def normalise(i, first):
                for q in range(2):
                    u = i * 2 + q
                    in_[q].wait(e, i, 16)
                    for t in range(UT):
                        ins = e.bn_stats(stats[q][:, t, :], x4[q][:, t, :])
                    ins.then_inc(stat.sem, 1)
                    stat.wait(e, u, 1)
                    apart(e, s_apart)
                    for t in range(UT):
                        ins = e.bn_aggr(mv[q][:, t, :], stats[q][:, t, :])
                    ins.then_inc(aggr.sem, 1)
                    root.wait(e, u, 1)
                    e.reciprocal(rstd[q][:], std[q][:]).then_inc(rec.sem, 1)
                    rec.wait(e, u, 1)
                    if not first:
                        out_[q].wait(e, i - 1, 16)
                        tr.wait(e, u - 2, 1)
                    for t in range(UT):
                        ins = e.tensor_scalar(xn4[q][:, t, :], x4[q][:, t, :], mv[q][:, t, 0:1], rstd[q][:, t:t + 1],
                                              ALU.subtract, ALU.mult)
                    ins.then_inc(norm.sem, 1)
                    lg.wait(e, u, 1)
                    e.tensor_copy(logits[:, bass.ds(u * UT, UT), :], pL[q][:]).then_inc(lgc.sem, 1)

            normalise(0, True)
            with e.Fori(1, HALF) as i:
                normalise(i, False)

        @block.tensor
        def _(e):
            e.wait_ge(s_wg, 16)

            def unit(i, first):
                for q in range(2):
                    u = i * 2 + q
                    norm.wait(e, u, 1)
                    for t in range(UT):
                        for m in range(MC):
                            b = t * MC + m
                            ins = e.transpose(pT[q][:, b // 4, (b % 4) * P:(b % 4 + 1) * P],
                                              xn4[q][:, t, m * P:(m + 1) * P], k["ident"][:])
                    ins.then_inc(tr.sem, 1)
                    trc.wait(e, u, 1)
                    if not first:
                        lgc.wait(e, u - 2, 1)
                    for t in range(UT):
                        for m in range(MC):
                            ins = e.matmul(pL[q][:, t, :], xT[q][:, t * MC + m, :], wg_sb[:, m, :],
                                           start=(m == 0), stop=(m == MC - 1))
                    ins.then_inc(lg.sem, 1)

            unit(0, True)
            with e.Fori(1, HALF) as i:
                unit(i, False)


def route(nc, k, logits, pick, slot_token):
    E = EXPERTS
    with ExitStack() as c:
        sb = lambda n, s, d=F32: c.enter_context(nc.sbuf_tensor(n, s, d))
        sem = lambda n: c.enter_context(nc.semaphore(n))
        shape = [P, TILES, E]
        ex, score, w, tmp = (sb(n, shape) for n in ("ex", "score", "w", "tmp"))
        ramp, eidx = sb("ramp", shape), sb("eidx", shape)
        hot = [sb(f"hot{i}", shape) for i in range(2)]
        hotb = [sb(f"hotb{i}", [P, E, TILES], BF16) for i in range(2)]
        top = sb("top", [P, 2, TILES])
        mx, tot = sb("mx", [P, TILES]), sb("tot", [P, TILES])
        rank = sb("rank", [P, E, TILES])
        cnt = [sb(f"cnt{i}", [P, E, TILES]) for i in range(2)]
        run = [sb(f"run{i}", [P, E, TILES]) for i in range(2)]
        zeros = sb("zeros", [P, TILES])
        pos, val, col, col2, spill = (sb(n, [P, TILES]) for n in ("pos", "val", "col", "col2", "spill"))
        tok = sb("tok", [P, TILES], mybir.dt.int32)
        tokf = sb("tokf", [P, TILES])
        put = [sb(f"put{i}", [P, TILES, 2], U32) for i in range(2)]
        stage = [sb(f"stage{i}", [P, 2, 2], U32) for i in range(2)]
        zero_u = sb("zero_u", [P, 2 * SLOTS // P], U32)
        pW = [c.enter_context(nc.psum_tensor(f"pW{i}", [P, E, TILES], F32)) for i in range(2)]
        pN = [c.enter_context(nc.psum_tensor(f"pN{i}", [P, E, TILES], F32)) for i in range(2)]
        s_iota, s_chain, s_exp, s_hot, s_cnt, s_put, s_zero, s_zset = (
            sem(n) for n in ("s_iota", "s_chain", "s_exp", "s_hot", "s_cnt", "s_put", "s_zero", "s_zset"))
        s_max, s_apart = sem("s_rmax"), sem("s_apart_route")
        staged = [Count(sem(f"s_staged{i}"), 1) for i in range(2)]
        sent = [Count(sem(f"s_sent{i}"), 32) for i in range(2)]
        block = c.enter_context(nc.Block())
        flat = lambda t: t[:].rearrange("p a b -> p (a b)")

        @block.sync
        def _(e):
            e.wait_ge(s_zset, 1)
            e.dma_start(slot_token.rearrange("(p n) o -> p (n o)", p=P), zero_u[:]).then_inc(s_zero, 16)
            e.wait_ge(s_zero, 16)

        @block.gpsimd
        def _(e):
            e.iota(tok[:], [[P, TILES]], base=0, channel_multiplier=1)
            e.iota(eidx[:], [[0, TILES], [1, E]], base=0, channel_multiplier=0, allow_small_or_imprecise_dtypes=True)
            e.iota(ramp[:], [[0, TILES], [-1, E]], base=E, channel_multiplier=0,
                   allow_small_or_imprecise_dtypes=True).then_inc(s_iota, 1)
            e.wait_ge(s_put, 1)
            e.wait_ge(s_zero, 16)

            def scatter(i, first):
                for q in range(2):
                    t = i * 2 + q
                    if not first:
                        sent[q].wait(e, i - 1, 32)
                    for j in range(2):
                        ins = e.tensor_copy(stage[q][:, j, :], put[j][:, bass.ds(t, 1), :].rearrange("p a b -> p (a b)"))
                    ins.then_inc(staged[q].sem, 1)
                    staged[q].wait(e, i, 1)
                    apart(e, s_apart)
                    for j in range(2):
                        e.indirect_dma_start(slot_token, bass.IndirectOffsetOnAxis(ap=stage[q][:, j, 0:1], axis=0),
                                             stage[q][:, j, 1:2], None).then_inc(sent[q].sem, 16)

            scatter(0, True)
            with e.Fori(1, TILES // 2) as i:
                scatter(i, False)
            for q in range(2):
                sent[q].wait(e, TILES // 2 - 1, 32)

        @block.scalar
        def _(e):
            e.wait_ge(s_max, 1)
            e.activation(flat(ex), flat(w), ACT.Exp).then_inc(s_exp, 1)

        @block.vector
        def _(e):
            done = [0]

            def chain(ins):
                done[0] += 1
                ins.then_inc(s_chain, 1)
                e.wait_ge(s_chain, done[0])

            spread = lambda t: t[:, :, None].broadcast_to(shape) if hasattr(t, "broadcast_to") else t
            wide = lambda t: t[:].rearrange("p (t o) -> p t o", o=1).to_broadcast(shape)
            e.memset(zero_u[:], 0).then_inc(s_zset, 1)
            e.memset(zeros[:], 0.0)
            chain(e.tensor_reduce(mx[:], logits[:], AX.X, ALU.max))
            e.tensor_tensor(w[:], logits[:], wide(mx), ALU.subtract).then_inc(s_max, 1)
            e.wait_ge(s_exp, 1)
            chain(e.tensor_reduce(tot[:], ex[:], AX.X, ALU.add))
            chain(e.reciprocal(mx[:], tot[:]))
            chain(e.tensor_tensor(score[:], ex[:], wide(mx), ALU.mult))
            e.wait_ge(s_iota, 1)
            for j in range(2):
                chain(e.tensor_reduce(top[:, j, :], score[:], AX.X, ALU.max))
                chain(e.tensor_tensor(w[:], score[:], top[:, j, :].rearrange("p (t o) -> p t o", o=1).to_broadcast(shape), ALU.is_equal))
                chain(e.tensor_tensor(w[:], w[:], ramp[:], ALU.mult))
                chain(e.tensor_reduce(mx[:], w[:], AX.X, ALU.max))
                chain(e.tensor_tensor(hot[j][:], w[:], wide(mx), ALU.is_equal))
                chain(e.tensor_copy(hotb[j][:].rearrange("p e t -> p t e"), hot[j][:]))
                if j == 0:
                    chain(e.scalar_tensor_tensor(score[:], hot[0][:], -4.0, score[:], ALU.mult, ALU.add))
            e.nop().then_inc(s_hot, 1)
            chain(e.tensor_tensor(tot[:], top[:, 0, :], top[:, 1, :], ALU.add))
            chain(e.reciprocal(mx[:], tot[:]))
            chain(e.tensor_tensor(top[:, 0, :], top[:, 0, :], mx[:], ALU.mult))
            chain(e.tensor_tensor(top[:, 1, :], top[:, 1, :], mx[:], ALU.mult))
            chain(e.tensor_copy(tokf[:], tok[:]))
            e.wait_ge(s_cnt, 1)
            for j in range(2):
                chain(e.tensor_copy(cnt[j][:], pN[j][:]))
                for x in range(E):
                    init = 0.0 if j == 0 else run[0][:, x, TILES - 1:TILES]
                    ins = e.tensor_tensor_scan(run[j][:, x, :], cnt[j][:, x, :], zeros[:], init, ALU.add, ALU.add)
                chain(ins)
                chain(e.tensor_tensor(rank[:], run[j][:], cnt[j][:], ALU.subtract))
                chain(e.tensor_tensor(rank[:], rank[:], pW[j][:], ALU.add))
                chain(e.tensor_tensor(w[:], rank[:].rearrange("p e t -> p t e"), hot[j][:], ALU.mult))
                chain(e.tensor_reduce(pos[:], w[:], AX.X, ALU.add))
                chain(e.tensor_scalar(val[:], pos[:], float(CAP), None, ALU.is_lt))
                chain(e.tensor_tensor(pos[:], pos[:], val[:], ALU.mult))
                chain(e.tensor_tensor(w[:], hot[j][:], eidx[:], ALU.mult))
                chain(e.tensor_reduce(col[:], w[:], AX.X, ALU.add))
                chain(e.scalar_tensor_tensor(col[:], col[:], float(CAP), pos[:], ALU.mult, ALU.add))
                chain(e.tensor_copy(pick[:, :, j], col[:]))
                chain(e.tensor_tensor(pick[:, :, 2 + j].bitcast(F32), top[:, j, :], val[:], ALU.mult))
                chain(e.tensor_scalar(spill[:], tokf[:], float(SLOTS + j * TOKENS), None, ALU.add))
                chain(e.tensor_tensor(col2[:], col[:], spill[:], ALU.subtract))
                chain(e.tensor_tensor(col2[:], col2[:], val[:], ALU.mult))
                chain(e.tensor_tensor(col2[:], col2[:], spill[:], ALU.add))
                chain(e.tensor_copy(put[j][:, :, 0], col2[:]))
                chain(e.tensor_copy(put[j][:, :, 1], tokf[:]))
            e.nop().then_inc(s_put, 1)

        @block.tensor
        def _(e):
            e.wait_ge(s_hot, 1)
            for j in range(2):
                e.matmul(flat(pW[j]), k["upper"][:], flat(hotb[j]), start=True, stop=True)
                ins = e.matmul(flat(pN[j]), k["ones"][:], flat(hotb[j]), start=True, stop=True)
            ins.then_inc(s_cnt, 1)


def experts(nc, k, xn_dram, slot_token, w1, b1, w2, b2, y_dram):
    GS = 512
    GROUPS = SLOTS // GS
    PER = CAP // GS
    GT = GS // P
    with ExitStack() as c:
        sb = lambda n, s, d=F32: c.enter_context(nc.sbuf_tensor(n, s, d))
        ps = lambda n, s: c.enter_context(nc.psum_tensor(n, s, F32))
        sem = lambda n: c.enter_context(nc.semaphore(n))
        two = lambda f: [f(i) for i in range(2)]
        idx = two(lambda i: sb(f"idx{i}", [P, GT], U32))
        xg = two(lambda i: sb(f"xg{i}", [P, GT, MODEL]))
        xh = two(lambda i: sb(f"xh{i}", [P, MC, GS], F32R))
        xl = two(lambda i: sb(f"xl{i}", [P, MC, GS], F32R))
        w1r, w2r = sb("w1r", [P, MC, HIDDEN]), sb("w2r", [P, HC, MODEL])
        w1h, w1l = (two(lambda i: sb(f"w1{n}{i}", [P, MC, HIDDEN], F32R)) for n in "hl")
        w2h, w2l = (two(lambda i: sb(f"w2{n}{i}", [P, HC, MODEL], F32R)) for n in "hl")
        b1r, b1T = sb("b1r", [EXPERTS * HC, P]), sb("b1T", [P, EXPERTS * HC])
        b1c = two(lambda i: sb(f"b1c{i}", [P, HC]))
        b2c = two(lambda i: sb(f"b2c{i}", [P, MODEL]))
        h32 = two(lambda i: sb(f"h32_{i}", [P, GS]))
        hh = two(lambda i: sb(f"hh{i}", [P, HC, GS], F32R))
        hl = two(lambda i: sb(f"hl{i}", [P, HC, GS], F32R))
        yb = [sb(f"yb{i}", [P, MODEL]) for i in range(GT)]
        pX = two(lambda i: ps(f"pX{i}", [P, GS]))
        pH = [ps(f"pH{i}", [P, GS]) for i in range(4)]
        pY = two(lambda i: ps(f"pY{i}", [P, MODEL]))
        s_b1, s_b1t, s_b1c0 = sem("s_b1"), sem("s_b1t"), sem("s_b1c0")
        s_apart = two(lambda i: sem(f"s_apart_ffn{i}"))
        wload = Count(sem("s_wload"), 48)
        whi = Count(sem("s_whi"), 2)
        wlo = Count(sem("s_wlo"), 2)
        bias = Count(sem("s_bias"), 1)
        ixl = two(lambda i: Count(sem(f"s_ix{i}"), 16))
        gat = two(lambda i: Count(sem(f"s_gat{i}"), 16 * GT))
        tX = Count(sem("s_tX"), 1)
        xhi, xlo = Count(sem("s_xhi"), 1), Count(sem("s_xlo"), 1)
        fH = Count(sem("s_fH"), HC)
        rl = Count(sem("s_rl"), HC)
        hhi = Count(sem("s_hhi"), HC)
        hlo = Count(sem("s_hlo"), HC)
        fY = Count(sem("s_fY"), GT)
        yv = Count(sem("s_yv"), GT)
        yst = [Count(sem(f"s_yst{i}"), 16) for i in range(GT)]
        block = c.enter_context(nc.Block())
        NE = EXPERTS // 2
        row = lambda v, e: v[bass.ds(e, 1)]

        def loop(eng, body):
            body(0, True, False)
            with eng.Fori(1, NE - 1) as i:
                body(i, False, False)
            body(NE - 1, False, True)

        st_v = slot_token.rearrange("(s t p) o -> s p (t o)", t=GT, p=P)
        w1v = w1.rearrange("e (c p) h -> e p c h", p=P)
        w2v = w2.rearrange("e (c p) m -> e p c m", p=P)
        yv_d = y_dram.rearrange("(s p) m -> s p m", p=P)

        @block.sync
        def _(e):
            def load_idx(sg, q):
                e.dma_start(idx[q][:], row(st_v, sg).rearrange("s p t -> (s p) t")).then_inc(ixl[q].sem, 16)

            def load_w(x, q):
                e.dma_start(w1r[:], row(w1v, x).rearrange("e p c h -> (e p) c h")).then_inc(wload.sem, 16)
                e.dma_start(w2r[:], row(w2v, x).rearrange("e p c h -> (e p) c h")).then_inc(wload.sem, 16)
                e.dma_start(b2c[q][:], row(b2, x).to_broadcast([P, MODEL])).then_inc(wload.sem, 16)

            with nc.allow_non_contiguous_dma(reason="slots' tokens, 4 bytes to a partition"):
                load_idx(0, 0)
                load_w(0, 0)
                e.dma_start(b1r[:], b1.rearrange("e (h p) -> (e h) p", p=P)).then_inc(s_b1, 16)
                load_idx(1, 1)

                def body(i, first, last):
                    for par in range(2):
                        x = 2 * i + par
                        for g in range(PER):
                            sg, q = PER * x + g, g % 2
                            if not (last and par == 1 and g >= PER - 2):
                                gat[q].wait(e, sg // 2 if isinstance(sg, int) else i * PER + (par * PER + g) // 2, 16 * GT)
                                apart(e, s_apart[1])
                                load_idx(sg + 2, q)
                            if g == 0 and not (last and par == 1):
                                wlo.wait(e, x, 2)
                                if not (first and par == 0):
                                    apart(e, s_apart[1])
                                    yv.wait(e, sg, 0)
                                apart(e, s_apart[1])
                                load_w(x + 1, 1 - par)
                            for t in range(GT):
                                if first and par == 0 and g == 0:
                                    continue
                                yv.wait(e, sg - 1, t + 1)
                                apart(e, s_apart[1])
                                e.dma_start(row(yv_d, (sg - 1) * GT + t).rearrange("s p m -> (s p) m"), yb[t][:]).then_inc(yst[t].sem, 16)

                loop(e, body)
            for t in range(GT):
                yv.wait(e, GROUPS - 1, t + 1)
                e.dma_start(yv_d[(GROUPS - 1) * GT + t], yb[t][:]).then_inc(yst[t].sem, 16)
            for t in range(GT):
                yst[t].wait(e, GROUPS - 1, 16)

        @block.gpsimd
        def _(e):
            def gather(sg, half, q, first=False):
                if not first:
                    tX.wait(e, sg - 2, 1)
                ixl[q].wait(e, half, 16)
                apart(e, s_apart[0])
                for t in range(GT):
                    e.indirect_dma_start(xg[q][:, t, :], None, xn_dram,
                                         bass.IndirectOffsetOnAxis(ap=idx[q][:, t:t + 1], axis=0)).then_inc(gat[q].sem, 16)

            def split(x, q):
                wload.wait(e, x, 48)
                apart(e, s_apart[0])
                for raw, hi in ((w1r, w1h[q]), (w2r, w2h[q])):
                    e.tensor_scalar(hi[:].rearrange("p a b -> p (a b)"), raw[:].rearrange("p a b -> p (a b)"), 1.0, 1.0,
                                    ALU.mult, ALU.mult).then_inc(whi.sem, 1)

            gather(0, 0, 0, True)
            split(0, 0)
            gather(1, 0, 1, True)

            def body(i, first, last):
                for par in range(2):
                    x = 2 * i + par
                    for g in range(PER):
                        sg = PER * x + g
                        if not (last and par == 1 and g >= PER - 2):
                            gather(sg + 2, i * PER + (par * PER + g) // 2 + 1, g % 2)
                        if g == 1 and not (last and par == 1):
                            fY.wait(e, sg - 1, 0)
                            split(x + 1, 1 - par)

            loop(e, body)

        @block.tensor
        def _(e):
            def rows(sg, half, q, first=False):
                gat[q].wait(e, half, 16 * GT)
                if not first:
                    xhi.wait(e, sg - 1, 1)
                    xlo.wait(e, sg - 1, 1)
                for m in range(MC):
                    for t in range(GT):
                        ins = e.transpose(pX[m][:, t * P:(t + 1) * P], xg[q][:, t, m * P:(m + 1) * P], k["ident"][:])
                ins.then_inc(tX.sem, 1)

            def up(sg, par, q, hc, first):
                if hc == 0:
                    xhi.wait(e, sg, 1)
                    xlo.wait(e, sg, 1)
                if not (first and hc < 4):
                    rl.wait(e, sg, hc - 3)
                ws = slice(hc * P, (hc + 1) * P)
                terms = [(w1h, xh), (w1h, xl), (w1l, xh)]
                n = 0
                for m in range(MC):
                    for w, xx in terms:
                        ins = e.matmul(pH[hc % 4][:], w[par][:, m, ws], xx[q][:, m, :], start=(n == 0), stop=(n == 3 * MC - 1))
                        n += 1
                ins.then_inc(fH.sem, 1)

            def down(sg, par, q, t, first):
                if t == 0:
                    hlo.wait(e, sg, HC)
                if not (first and t < 2):
                    yv.wait(e, sg, t - 1)
                ts_ = slice(t * P, (t + 1) * P)
                for hc in range(HC):
                    for n, (hs, ws) in enumerate(((hh, w2h), (hh, w2l), (hl, w2h))):
                        ins = e.matmul(pY[t % 2][:], hs[q][:, hc, ts_], ws[par][:, hc, :],
                                       start=(hc == 0 and n == 0), stop=(hc == HC - 1 and n == 2))
                ins.then_inc(fY.sem, 1)

            e.wait_ge(s_b1, 16)
            e.transpose(pY[0][:, 0:EXPERTS * HC], b1r[:], k["ident"][0:EXPERTS * HC, 0:EXPERTS * HC]).then_inc(s_b1t, 1)
            rows(0, 0, 0, True)
            e.wait_ge(s_b1c0, 1)

            def body(i, first, last):
                for par in range(2):
                    x = 2 * i + par
                    for g in range(PER):
                        sg = PER * x + g
                        start = first and par == 0 and g == 0
                        if g == 0:
                            wlo.wait(e, x, 2)
                        for hc in range(HC):
                            up(sg, par, g % 2, hc, start)
                            if hc == 2 and not (last and par == 1 and g == PER - 1):
                                rows(sg + 1, i * PER + (par * PER + g + 1) // 2, (g + 1) % 2)
                            if hc % 2 and not start:
                                down(sg - 1, par if g else 1 - par, (g + 1) % 2, hc // 2,
                                     first and par == 0 and g == 1)

            loop(e, body)
            for t in range(GT):
                down(GROUPS - 1, 1, 1, t, False)

        @block.scalar
        def _(e):
            def rows(sg, q, first=False):
                tX.wait(e, sg, 1)
                if not first:
                    fH.wait(e, sg - 2, HC)
                for m in range(MC):
                    ins = e.activation(xh[q][:, m, :], pX[m][:], ACT.Copy)
                ins.then_inc(xhi.sem, 1)

            e.wait_ge(s_b1t, 1)
            e.activation(b1T[:], pY[0][:, 0:EXPERTS * HC], ACT.Copy).then_inc(s_b1c0, 1)
            rows(0, 0, True)

            def body(i, first, last):
                for par in range(2):
                    x = 2 * i + par
                    e.wait_ge(s_b1c0, 1)
                    e.activation(b1c[par][:], b1T[:, bass.ds(x * HC, HC)], ACT.Copy).then_inc(bias.sem, 1)
                    bias.wait(e, x, 1)
                    for g in range(PER):
                        sg, q = PER * x + g, g % 2
                        start = first and par == 0 and g == 0
                        for hc in range(HC):
                            fH.wait(e, sg, hc + 1)
                            if not (start and hc < 2):
                                hlo.wait(e, sg, hc - 1)
                            e.activation(h32[hc % 2][:], pH[hc % 4][:], ACT.Relu, bias=b1c[par][:, hc:hc + 1]).then_inc(rl.sem, 1)
                            rl.wait(e, sg, hc + 1)
                            if hc == 0 and not (first and par == 0 and g < 2):
                                fY.wait(e, sg - 2, GT)
                            e.activation(hh[q][:, hc, :], h32[hc % 2][:], ACT.Copy).then_inc(hhi.sem, 1)
                            if hc == 2 and not (last and par == 1 and g == PER - 1):
                                rows(sg + 1, (g + 1) % 2, start)

            loop(e, body)

        @block.vector
        def _(e):
            def rows(sg, q):
                xhi.wait(e, sg, 1)
                for m in range(MC):
                    ins = e.tensor_tensor(xl[q][:, m, :], pX[m][:], xh[q][:, m, :].bitcast(F32), ALU.subtract)
                ins.then_inc(xlo.sem, 1)

            def split(x, q, j):
                raw, hi, lo = ((w1r, w1h[q], w1l[q]), (w2r, w2h[q], w2l[q]))[j]
                whi.wait(e, x, j + 1)
                e.tensor_tensor(lo[:], raw[:], hi[:].bitcast(F32), ALU.subtract).then_inc(wlo.sem, 1)

            def down(sg, par, t, first):
                fY.wait(e, sg, t + 1)
                if not first:
                    yst[t].wait(e, sg - 1, 16)
                e.tensor_tensor(yb[t][:], pY[t % 2][:], b2c[par][:], ALU.add).then_inc(yv.sem, 1)

            split(0, 0, 0)
            split(0, 0, 1)
            rows(0, 0)

            def body(i, first, last):
                for par in range(2):
                    x = 2 * i + par
                    for g in range(PER):
                        sg, q = PER * x + g, g % 2
                        start = first and par == 0 and g == 0
                        for hc in range(HC):
                            hhi.wait(e, sg, hc + 1)
                            e.tensor_tensor(hl[q][:, hc, :], h32[hc % 2][:], hh[q][:, hc, :].bitcast(F32),
                                            ALU.subtract).then_inc(hlo.sem, 1)
                            if hc == 2 and not (last and par == 1 and g == PER - 1):
                                rows(sg + 1, (g + 1) % 2)
                            if hc % 2 and not start:
                                down(sg - 1, par if g else 1 - par, hc // 2, first and par == 0 and g == 1)
                            if g == 2 and hc in (4, 6) and not (last and par == 1):
                                split(x + 1, 1 - par, hc // 2 - 2)

            loop(e, body)
            for t in range(GT):
                down(GROUPS - 1, 1, t, False)


def attention_and_sum(nc, k, x, xn_dram, w_qkv, w_out, pick, y_dram, out):
    UNITS = BATCH * PAIRS
    STEPS, LAG, RING = 2 * QT, 3, 4
    HALF = 512
    HT = HALF // P
    GQ = 2 * P
    GROUPS = SEQ // GQ
    AHEAD = QT + 1
    width = lambda s: (s // 2 + 1) * P
    shift = lambda s: P if width(s) == HALF + P else 0
    CH = [[b for b in (min(HT, s // 2 + 1), s // 2 + 1 - HT) if b > 0] for s in range(STEPS)]
    FIRST_CH = [sum(len(x) for x in CH[:s]) for s in range(STEPS + 1)]
    CHUNKS = FIRST_CH[STEPS]
    assert all(FIRST_CH[4 * g] % 2 == 0 for g in range(GROUPS + 1)) and STEPS % RING == 0

    FULL = ["q0", "q1", "k0", "k1", "v0", "t0", "v1", "t1", "xn", "o0", "o1", "o2", "o3"]
    STEP_OF = {p: i for i, p in enumerate(FULL)}
    BEFORE, FIRST, TAIL = FULL[:8], FULL[:9], FULL[9:]
    BY_ACT = {"q0", "q1", "k0", "k1", "v0", "v1", "xn"}
    BY_DVE = {"q0", "q1", "k0", "k1", "t0", "t1", "xn", "o0", "o1", "o2", "o3"}

    def pieces(n):
        if isinstance(n, int):
            return BEFORE if n < 0 else FIRST if n == 0 else TAIL if n >= UNITS - 1 else FULL
        return FULL

    class Pieces:

        def __init__(self, sem_, own):
            self.sem, self.own = sem_, own
            self.of = lambda names: sum(x in own for x in names)

        def wait(self, eng, n, name=None):
            if isinstance(n, int):
                v = sum(self.of(pieces(m)) for m in range(-1, n))
            else:
                v = n * self.of(FULL) + (self.of(BEFORE) + self.of(FIRST) - self.of(FULL))
            if name is not None:
                names = pieces(n)
                v = v + self.of(names[:names.index(name) + 1])
            eng.wait_ge(self.sem, v)

    with ExitStack() as c:
        sb = lambda n, s, d=F32: c.enter_context(nc.sbuf_tensor(n, s, d))
        ps = lambda n, s: c.enter_context(nc.psum_tensor(n, s, F32))
        sem = lambda n: c.enter_context(nc.semaphore(n))
        two = lambda f: [f(i) for i in range(2)]
        qh, ql = (two(lambda i: two(lambda h: sb(f"q{n}{i}{h}", [P, SEQ], F32R))) for n in "hl")
        kk = two(lambda i: two(lambda h: sb(f"kk{i}{h}", [P, SEQ], F32R)))
        vv = two(lambda i: sb(f"vv{i}", [P, QT, P]))
        vT = sb("vT", [P, HALF])
        pT = two(lambda h: two(lambda g: sb(f"pT{h}{g}", [P, QT - 2 + 2 * g, GQ])))
        pr = [sb(f"pr{i}", [P, SEQ]) for i in range(RING)]
        negm, rsum, rinv = (sb(n, [P, RING]) for n in ("negm", "rsum", "rinv"))
        oh, ol = (two(lambda i: sb(f"o{n}{i}", [P, SEQ], F32R)) for n in "hl")
        xnh, xnl = (sb(f"xn{n}", [P, 2 * QT, MC, P], F32R) for n in "hl")
        xnt = sb("xnt", [P, MODEL])
        wr = sb("wr", [P, MC, 2, 3 * HDIM])
        wh, wl = (sb(f"w{n}", [P, MC, 3, 2, HDIM], F32R) for n in "hl")
        woh, wol = (sb(f"wo{n}", [P, PAIRS, MODEL], F32R) for n in "hl")
        res = sb("res", [P, 2 * QT, MODEL])
        yg = two(lambda j: sb(f"yg{j}", [P, MODEL]))
        sel = sb("sel", [P, 4], U32)
        ot = two(lambda i: sb(f"ot{i}", [P, MODEL]))
        S = two(lambda i: ps(f"S{i}", [P, SEQ]))
        T = two(lambda i: ps(f"T{i}", [P, HALF]))
        O = ps("O", [P, GQ])
        W = ps("W", [P, HALF])

        row = lambda v, i: v[bass.ds(i, 1)]
        flat = lambda t: t.rearrange("p a b -> p (a b)")

        def split_weights(e, s_hi, wait_hi, s_lo):
            raw = lambda m: wr[:, m].rearrange("p h (w d) -> p h w d", d=HDIM)
            put = lambda t, m: t[:, m].rearrange("p w h d -> p h w d")
            for m in range(MC):
                ins = e.tensor_scalar(put(wh, m), raw(m), 1.0, 1.0, ALU.mult, ALU.mult)
            ins.then_inc(s_hi, 1)
            wait_hi()
            for m in range(MC):
                ins = e.tensor_tensor(put(wl, m), raw(m), put(wh, m).bitcast(F32), ALU.subtract)
            ins.then_inc(s_lo, 1)

        xv = x.rearrange("b (t p) m -> (b t) p m", p=P)
        outv = out.rearrange("b (t p) m -> (b t) p m", p=P)
        xnv = xn_dram.rearrange("(t p) m -> t p m", p=P)
        wv = w_qkv.rearrange("(c p) (g h) d -> g p c (h d)", p=P, h=2)
        wov = w_out.rearrange("(g h) d m -> (h d) g m", h=2)

        with ExitStack() as pre:
            psem = lambda n: pre.enter_context(nc.semaphore(n))
            s_wo, s_wohi, s_wolo, s_res0, s_w0, s_w0hi, s_w0lo = (
                psem(n) for n in ("s_wo", "s_wohi", "s_wolo", "s_res0", "s_w0", "s_w0hi", "s_w0lo"))
            s_xn = [psem(f"s_xn{i}") for i in range(4)]
            s_tr, s_hi, s_lo = (psem(n) for n in ("s_ptr", "s_phi", "s_plo"))
            wo_raw = res[:, QT:2 * QT, :]
            ring = [pr[i][:, 0:MODEL] for i in range(4)]
            bank = [T[0], T[1], W, S[0]]
            block = pre.enter_context(nc.Block())

            @block.sync
            def _(e):
                for t in range(AHEAD):
                    if t >= 4:
                        e.wait_ge(s_tr, t - 3)
                    e.dma_start(ring[t % 4], xnv[t]).then_inc(s_xn[t % 4], 16)
                    if t == 1:
                        e.dma_start(wr[:].rearrange("p c h d -> p c (h d)"), wv[0]).then_inc(s_w0, 16)
                        e.dma_start(wo_raw, wov).then_inc(s_wo, 16)
                        e.dma_start(res[:, 0:QT, :], x[0].rearrange("(t p) m -> p t m", p=P)).then_inc(s_res0, 16)
                e.wait_ge(s_res0, 16)

            @block.tensor
            def _(e):
                for t in range(AHEAD):
                    e.wait_ge(s_xn[t % 4], 16 * (t // 4 + 1))
                    if t >= 4:
                        e.wait_ge(s_lo, t - 3)
                    for m in range(MC):
                        ins = e.transpose(bank[t % 4][:, m * P:(m + 1) * P], ring[t % 4][:, m * P:(m + 1) * P], k["ident"][:])
                    ins.then_inc(s_tr, 1)

            @block.scalar
            def _(e):
                for t in range(AHEAD):
                    e.wait_ge(s_tr, t + 1)
                    e.activation(flat(xnh[:, t]), bank[t % 4][:, 0:MODEL], ACT.Copy).then_inc(s_hi, 1)

            @block.vector
            def _(e):
                for t in range(AHEAD):
                    e.wait_ge(s_hi, t + 1)
                    e.tensor_tensor(flat(xnl[:, t]), bank[t % 4][:, 0:MODEL], flat(xnh[:, t]).bitcast(F32),
                                    ALU.subtract).then_inc(s_lo, 1)
                e.wait_ge(s_wohi, 1)
                e.tensor_tensor(wol[:], wo_raw, woh[:].bitcast(F32), ALU.subtract).then_inc(s_wolo, 1)

            @block.gpsimd
            def _(e):
                e.wait_ge(s_w0, 16)
                split_weights(e, s_w0hi, lambda: e.wait_ge(s_w0hi, 1), s_w0lo)
                e.wait_ge(s_wo, 16)
                e.tensor_scalar(woh[:], wo_raw, 1.0, 1.0, ALU.mult, ALU.mult).then_inc(s_wohi, 1)

        score = Count(sem("s_score"), STEPS)
        negmax = Count(sem("s_negmax"), STEPS)
        expd = Count(sem("s_expd"), STEPS)
        recip = Count(sem("s_recip"), STEPS)
        scaled = Count(sem("s_scaled"), STEPS)
        turned = Count(sem("s_turned"), CHUNKS)
        kept = two(lambda i: Count(sem(f"s_kept{i}"), CHUNKS // 2))
        pv = Count(sem("s_pv"), GROUPS)
        ohi, olo = Count(sem("s_ohi"), GROUPS), Count(sem("s_olo"), GROUPS)
        filled = Pieces(sem("s_filled"), set(FULL))
        act = Pieces(sem("s_act"), BY_ACT)
        dve = Pieces(sem("s_dve"), BY_DVE)
        dup = Count(sem("s_dup"), 64)
        wload = Count(sem("s_wload_a"), 16)
        whi, wlo = Count(sem("s_whi_a"), 1), Count(sem("s_wlo_a"), 1)
        xload = Count(sem("s_xload"), 16)
        rload = Count(sem("s_rload"), 16)
        picked = Count(sem("s_picked"), 1)
        ygot = Count(sem("s_ygot"), 32)
        sum1, sum2, summed = (Count(sem(f"s_sum{i}"), 1) for i in range(3))
        stored = two(lambda i: Count(sem(f"s_stored{i}"), 16))
        s_apart = {n: sem(f"s_apart_{n}") for n in ("sp", "pool", "act")}
        ytail = sem("s_ytail")
        block = c.enter_context(nc.Block())

        def units(eng, unit):
            def pair(j, early, first=False, last=False):
                for q in range(2):
                    unit(2 * j + q, q, j, early, first and q == 0, last and q == 1)

            pair(0, True, first=True)
            with eng.Fori(1, QT // 2) as j:
                pair(j, True)
            with eng.Fori(QT // 2, UNITS // 2 - 1) as j:
                pair(j, False)
            pair(UNITS // 2 - 1, False, last=True)

        def lagged(n, q, s):
            return (n, q, s - LAG) if s >= LAG else (n - 1, 1 - q, s - LAG + STEPS)

        def group_at(n, q, s):
            t = s - LAG - 1
            n_, q_, t = (n, q, t) if t >= 0 else (n - 1, 1 - q, t + STEPS)
            return (n_, q_, t // 4) if t % 4 == 3 else None

        real = lambda n: not (isinstance(n, int) and n < 0)

        @block.sync
        def _(e):
            def load_w(n):
                e.dma_start(wr[:].rearrange("p c h d -> p c (h d)"),
                            row(wv, n % PAIRS).rearrange("g p c d -> (g p) c d")).then_inc(wload.sem, 16)

            def double(n, q):
                act.wait(e, n, "q1")
                apart(e, s_apart["sp"])
                dve.wait(e, n, "q1")
                apart(e, s_apart["sp"])
                for t in (qh, ql):
                    e.dma_start(t[q][0][HDIM:P, :].bitcast(F32), t[q][0][0:HDIM, :].bitcast(F32)).then_inc(dup.sem, 16)
                    e.dma_start(t[q][1][0:HDIM, :].bitcast(F32), t[q][1][HDIM:P, :].bitcast(F32)).then_inc(dup.sem, 16)

            load_w(1)
            double(-1, 0)
            wlo.wait(e, 0, 1)
            load_w(2)

            def unit(n, q, j, early, first, last):
                if not last:
                    if not first:
                        filled.wait(e, n - 1, "xn")
                        apart(e, s_apart["sp"])
                    e.dma_start(xnt[:], row(xnv, (n + AHEAD) % TILES).rearrange("t p m -> (t p) m")).then_inc(xload.sem, 16)
                    double(n, 1 - q)
                    if not (isinstance(n, int) and n > 1):
                        wlo.wait(e, n + 1, 1)
                        apart(e, s_apart["sp"])
                        load_w(n + 3)
                if not early:
                    summed.wait(e, n - QT, 1)
                    apart(e, s_apart["sp"])
                    e.dma_start(row(outv, n - QT).rearrange("t p m -> (t p) m"), ot[q][:]).then_inc(stored[q].sem, 16)
                if not (isinstance(n, int) and n > 1):
                    e.dma_start(flat(res[:, bass.ds((n + QT) % (2 * QT), 1), :]),
                                row(xv, (n + QT) % TILES).rearrange("t p m -> (t p) m")).then_inc(rload.sem, 16)

            units(e, unit)
            for t in range(QT):
                m = UNITS - QT + t
                summed.wait(e, m, 1)
                e.dma_start(outv[m], ot[m % 2][:]).then_inc(stored[m % 2].sem, 16)
            for q in range(2):
                stored[q].wait(e, TILES // 2 - 1, 16)

        @block.tensor
        def _(e):
            def project(n, name):
                w, f = "qkv".index(name[0]), int(name[1])
                if name == "q0" and real(n):
                    wlo.wait(e, n, 1)
                i = 0
                t0 = ((n + 1) // PAIRS) % 2 * QT + f * HT
                for m in range(MC):
                    for ws, xs in ((wh, xnh), (wh, xnl), (wl, xnh)):
                        ins = e.matmul(W[:], ws[:, m, w].rearrange("p h d -> p (h d)"), xs[:, bass.ds(t0, HT), m, :],
                                       start=(i == 0), stop=(i == 3 * MC - 1))
                        i += 1
                return ins

            def turn_v():
                for b in range(HT):
                    ins = e.transpose(W[:, b * P:(b + 1) * P], vT[:, b * P:(b + 1) * P], k["ident"][:])
                return ins

            def turn_xn(n):
                xload.wait(e, n, 16)
                for m in range(MC):
                    ins = e.transpose(W[:, m * P:(m + 1) * P], xnt[:, m * P:(m + 1) * P], k["ident"][:])
                return ins

            def out_project(n, q, j):
                if j == 0:
                    olo.wait(e, n, GROUPS)
                for t in range(2):
                    ts_ = slice((2 * j + t) * P, (2 * j + t + 1) * P)
                    for i, (os_, ws) in enumerate(((oh, woh), (oh, wol), (ol, woh))):
                        ins = e.matmul(W[:, t * MODEL:(t + 1) * MODEL], os_[q][:, ts_],
                                       flat(ws[:, bass.ds(n % PAIRS, 1), :]), start=(i == 0), stop=(i == 2))
                return ins

            def work(n, q, name):
                before = pieces(n)[:pieces(n).index(name)]
                last_by = lambda own: next((x for x in reversed(before) if x in own), None)
                if not (n == -1 and not before) if isinstance(n, int) else True:
                    if not before or before[-1] in BY_ACT:
                        act.wait(e, n, last_by(BY_ACT))
                    if not before or before[-1] in BY_DVE:
                        dve.wait(e, n, last_by(BY_DVE))
                if name[0] in "qkv":
                    ins = project(n, name)
                elif name[0] == "t":
                    ins = turn_v()
                elif name == "xn":
                    ins = turn_xn(n)
                else:
                    ins = out_project(n - 1, 1 - q, int(name[1]))
                ins.then_inc(filled.sem, 1)

            def scores(n, q, s, first):
                i, h = s // 2, s % 2
                if s == 0:
                    dup.wait(e, n, 64)
                    act.wait(e, n - 1, "k1")
                    dve.wait(e, n - 1, "k1")
                if not (first and s < 2):
                    expd.wait(e, n, s - 1)
                off, w = shift(s), max(width(s), 2 * P)
                cuts = [off] + [b for b in (HALF,) if off < b < off + w] + [off + w]
                for a, b in zip(cuts, cuts[1:]):
                    diag = off + i * P
                    here = a <= diag < b
                    for t in (qh, ql):
                        ins = e.matmul(S[s % 2][:, a:b], t[q][h][:, i * P:(i + 1) * P], kk[q][h][:, a - off:b - off],
                                       start=(t is qh), stop=(t is ql and not here))
                    if here:
                        ins = e.matmul(S[s % 2][:, diag:diag + P], k["identb"][:], k["mask"][:], start=False, stop=True)
                ins.then_inc(score.sem, 1)

            def turn_p(n, q, s):
                scaled.wait(e, n, s + 1)
                for i, blocks in enumerate(CH[s]):
                    ch = FIRST_CH[s] + i
                    if not (isinstance(n, int) and n == 0 and ch < 2):
                        kept[ch % 2].wait(e, n, ch // 2)
                    for b in range(blocks):
                        kt = i * HT + b
                        ins = e.transpose(T[ch % 2][:, b * P:(b + 1) * P], pr[s % RING][:, kt * P:(kt + 1) * P], k["ident"][:])
                    ins.then_inc(turned.sem, 1)

            def values(n, q, g):
                for i in range(2):
                    kept[i].wait(e, n, FIRST_CH[4 * g + 4] // 2)
                if g == 0:
                    dve.wait(e, n - 1, "t1")
                if not (isinstance(n, int) and n == 0 and g == 0):
                    olo.wait(e, n, g)
                KT = 2 * g + 2
                for kt in range(KT):
                    a = P if kt == KT - 1 else 0
                    for h in range(2):
                        hs = slice(h * HDIM, (h + 1) * HDIM)
                        ins = e.matmul(O[hs, a:GQ], vv[q][:, kt, hs], pT[h][g % 2][:, kt, a:GQ],
                                       start=(kt == 0), stop=(kt == KT - 1))
                ins.then_inc(pv.sem, 1)

            for name in BEFORE:
                work(-1, 1, name)

            def tail(n, q, s):
                n_, q_, s_ = lagged(n, q, s)
                if real(n_) and not (isinstance(n_, int) and n_ >= UNITS):
                    turn_p(n_, q_, s_)
                g = group_at(n, q, s)
                if g and real(g[0]):
                    values(*g)

            def unit(n, q, j, early, first, last):
                for s in range(STEPS):
                    scores(n, q, s, first)
                    for name in pieces(n):
                        if STEP_OF[name] == s:
                            work(n, q, name)
                    tail(n, q, s)

            units(e, unit)
            for s in range(LAG + 1):
                tail(UNITS, 0, s)
            for name in TAIL:
                work(UNITS, 0, name)

        def keep(e, n, s, parity):
            i, h = s // 2, s % 2
            g = i // 2
            for x, blocks in enumerate(CH[s]):
                ch = FIRST_CH[s] + x
                if ch % 2 != parity:
                    continue
                if s % 4 < 2 and not (isinstance(n, int) and n == 0 and g < 2):
                    pv.wait(e, n, g - 1)
                turned.wait(e, n, ch + 1)
                dst = pT[h][g % 2][:, x * HT:x * HT + blocks, (i % 2) * P:(i % 2 + 1) * P]
                src = T[ch % 2][:, 0:blocks * P].rearrange("p (b c) -> p b c", c=P)
                ins = e.activation(dst, src, ACT.Copy) if parity == 0 else e.tensor_copy(dst, src)
                ins.then_inc(kept[parity].sem, 1)

        @block.scalar
        def _(e):
            def softmax(n, q, s, first):
                i = s % RING
                m, t = (n, s - RING) if s >= RING else (n - 1, s - RING + STEPS)
                if real(m):
                    turned.wait(e, m, FIRST_CH[t + 1])
                negmax.wait(e, n, s + 1)
                off, w = shift(s), width(s)
                e.activation(pr[i][:, 0:w], S[s % 2][:, off:off + w], ACT.Exp, bias=negm[:, i:i + 1],
                             accum_out=rsum[:, i:i + 1]).then_inc(expd.sem, 1)

            def work(n, q, name):
                filled.wait(e, n, name)
                if name == "xn":
                    apart(e, s_apart["act"])
                    ins = e.activation(xnh[:, bass.ds((n + AHEAD) % (2 * QT), 1), :, :].rearrange("p t m c -> p (t m c)"),
                                       W[:, 0:MODEL], ACT.Copy)
                elif name[0] == "v":
                    ins = e.activation(vT[:], W[:], ACT.Copy)
                else:
                    cols = slice(int(name[1]) * HALF, (int(name[1]) + 1) * HALF)
                    dst, scale = (qh, QSCALE) if name[0] == "q" else (kk, 1.0)
                    for h in range(2):
                        hs = slice(h * HDIM, (h + 1) * HDIM)
                        ins = e.activation(dst[1 - q][h][hs, cols], W[hs, :], ACT.Copy, scale=scale)
                ins.then_inc(act.sem, 1)

            for name in BEFORE:
                if name in BY_ACT:
                    work(-1, 1, name)

            def tail(n, q, s):
                n_, q_, s_ = lagged(n, q, s)
                if real(n_) and not (isinstance(n_, int) and n_ >= UNITS):
                    keep(e, n_, s_, 0)
                g = group_at(n, q, s)
                if g and real(g[0]):
                    m, p_, g_ = g
                    pv.wait(e, m, g_ + 1)
                    e.activation(oh[p_][:, g_ * GQ:(g_ + 1) * GQ], O[:], ACT.Copy).then_inc(ohi.sem, 1)

            def unit(n, q, j, early, first, last):
                for s in range(STEPS):
                    softmax(n, q, s, first)
                    for name in pieces(n):
                        if STEP_OF[name] == s and name in BY_ACT:
                            work(n, q, name)
                    tail(n, q, s)

            units(e, unit)
            for s in range(LAG + 1):
                tail(UNITS, 0, s)

        @block.vector
        def _(e):
            def reciprocal(n, s):
                i = s % RING
                expd.wait(e, n, s + 1)
                e.reciprocal(rinv[:, i:i + 1], rsum[:, i:i + 1]).then_inc(recip.sem, 1)

            def work(n, q, name):
                if name in BY_ACT:
                    act.wait(e, n, name)
                else:
                    filled.wait(e, n, name)
                if name == "xn":
                    slot = bass.ds((n + AHEAD) % (2 * QT), 1)
                    ins = e.tensor_tensor(xnl[:, slot, :, :].rearrange("p t m c -> p (t m c)"), W[:, 0:MODEL],
                                          xnh[:, slot, :, :].rearrange("p t m c -> p (t m c)").bitcast(F32), ALU.subtract)
                elif name[0] == "t":
                    f = int(name[1])
                    ins = e.tensor_copy(flat(vv[1 - q][:, f * HT:(f + 1) * HT, :]), W[:])
                elif name[0] == "o":
                    if name == "o0" and real(n - 1 if isinstance(n, int) else n):
                        rload_wait(n)
                    at = ((n - 1) // PAIRS) % 2 * QT + 2 * int(name[1])
                    r = flat(res[:, bass.ds(at, 2), :])
                    ins = e.tensor_tensor(r, W[:], r, ALU.add)
                else:
                    cols = slice(int(name[1]) * HALF, (int(name[1]) + 1) * HALF)
                    for h in range(2):
                        hs, other = slice(h * HDIM, (h + 1) * HDIM), slice((1 - h) * HDIM, (2 - h) * HDIM)
                        if name[0] == "q":
                            ins = e.scalar_tensor_tensor(ql[1 - q][h][hs, cols], W[hs, :], QSCALE,
                                                         qh[1 - q][h][hs, cols].bitcast(F32), ALU.mult, ALU.subtract)
                        else:
                            ins = e.tensor_tensor(kk[1 - q][h][other, cols], W[hs, :],
                                                  kk[1 - q][h][hs, cols].bitcast(F32), ALU.subtract)
                ins.then_inc(dve.sem, 1)

            def rload_wait(n):
                if isinstance(n, int):
                    if n >= 2:
                        rload.wait(e, min(n - 2, UNITS - 2 - 1), 16)
                else:
                    rload.wait(e, n - 2, 16)

            for name in BEFORE:
                if name in BY_DVE:
                    work(-1, 1, name)

            def tail(n, q, s):
                n_, q_, s_ = lagged(n, q, s)
                if real(n_) and not (isinstance(n_, int) and n_ >= UNITS):
                    keep(e, n_, s_, 1)
                g = group_at(n, q, s)
                if g and real(g[0]):
                    m, p_, g_ = g
                    ohi.wait(e, m, g_ + 1)
                    cols = slice(g_ * GQ, (g_ + 1) * GQ)
                    e.tensor_tensor(ol[p_][:, cols], O[:], oh[p_][:, cols].bitcast(F32), ALU.subtract).then_inc(olo.sem, 1)

            def unit(n, q, j, early, first, last):
                for s in range(STEPS):
                    if s:
                        reciprocal(n, s - 1)
                    elif not first:
                        reciprocal(n - 1, STEPS - 1)
                    i = s % RING
                    score.wait(e, n, s + 1)
                    off, w = shift(s), width(s)
                    e.tensor_reduce(negm[:, i:i + 1], S[s % 2][:, off:off + w], AX.X, ALU.max,
                                    negate=True).then_inc(negmax.sem, 1)
                    for name in pieces(n):
                        if STEP_OF[name] == s and name in BY_DVE:
                            work(n, q, name)
                    tail(n, q, s)

            units(e, unit)
            reciprocal(UNITS - 1, STEPS - 1)
            for s in range(LAG + 1):
                tail(UNITS, 0, s)
            for name in TAIL:
                work(UNITS, 0, name)

        @block.gpsimd
        def _(e):
            def split(n):
                filled.wait(e, n, "v1")
                apart(e, s_apart["pool"])
                wload.wait(e, n + 1, 16)
                apart(e, s_apart["pool"])
                split_weights(e, whi.sem, lambda: whi.wait(e, n + 1, 1), wlo.sem)

            def fetch(m):
                if not (isinstance(m, int) and m == 0):
                    summed.wait(e, m - 1, 1)
                e.tensor_copy(sel[:], pick[:, bass.ds(m, 1), :].rearrange("p t c -> p (t c)")).then_inc(picked.sem, 1)
                picked.wait(e, m, 1)
                apart(e, s_apart["pool"])
                for j in range(TOPK):
                    e.indirect_dma_start(yg[j][:], None, y_dram,
                                         bass.IndirectOffsetOnAxis(ap=sel[:, j:j + 1], axis=0)).then_inc(ygot.sem, 16)

            def total(n, q):
                m = n - QT
                ygot.wait(e, m, 32)
                apart(e, s_apart["pool"])
                for j in range(TOPK):
                    ins = e.tensor_scalar(yg[j][:], yg[j][:], sel[:, 2 + j:3 + j].bitcast(F32), 1.0, ALU.mult, ALU.mult)
                ins.then_inc(sum1.sem, 1)
                sum1.wait(e, m, 1)
                e.tensor_tensor(yg[0][:], yg[0][:], yg[1][:], ALU.add).then_inc(sum2.sem, 1)
                sum2.wait(e, m, 1)
                apart(e, s_apart["pool"])
                if not (isinstance(m, int) and m < 2):
                    stored[q].wait(e, (m - q) // 2 - 1, 16)
                    apart(e, s_apart["pool"])
                dve.wait(e, n if not isinstance(n, int) else min(n, UNITS), "o3")
                e.tensor_tensor(ot[q][:], flat(res[:, bass.ds(m % (2 * QT), 1), :]), yg[0][:], ALU.add).then_inc(summed.sem, 1)

            split(-1)

            def unit(n, q, j, early, first, last):
                if not early:
                    fetch(n - QT)
                for s in range(STEPS):
                    i = s % RING
                    recip.wait(e, n, s + 1)
                    apart(e, s_apart["pool"])
                    e.tensor_scalar(pr[i][:, 0:width(s)], pr[i][:, 0:width(s)], rinv[:, i:i + 1], 1.0,
                                    ALU.mult, ALU.mult).then_inc(scaled.sem, 1)
                    if s == STEP_OF["v1"] + 2 and not (isinstance(n, int) and n > 1):
                        split(n)
                    if s == STEPS - 1 and not early:
                        total(n, q)

            units(e, unit)
            for t in range(QT):
                fetch(UNITS - QT + t)
                total(UNITS + t, t % 2)


def program(nc, x, w_qkv, w_out, wg, w1, b1, w2, b2, out):
    xn_dram = nc.dram_tensor("xn", (TOKENS, MODEL), F32).ap()
    y_dram = nc.dram_tensor("y", (SLOTS, MODEL), F32).ap()
    slot_token = nc.dram_tensor("slot_token", (2 * SLOTS, 1), U32).ap()
    with ExitStack() as c:
        k = constants(nc, c)
        pick = c.enter_context(nc.sbuf_tensor("pick", [P, TILES, 4], U32))
        with ExitStack() as c2:
            logits = c2.enter_context(nc.sbuf_tensor("logits", [P, TILES, EXPERTS], F32))
            layernorm_and_router(nc, k, x, wg, xn_dram, logits)
            route(nc, k, logits, pick, slot_token)
        experts(nc, k, xn_dram, slot_token, w1, b1, w2, b2, y_dram)
        attention_and_sum(nc, k, x, xn_dram, w_qkv, w_out, pick, y_dram, out)


_INS = ["L0_attn_x", "L0_attn_w_qkv", "L0_attn_w_out", "L0_ffn_wg", "L0_ffn_w1", "L0_ffn_b1", "L0_ffn_w2", "L0_ffn_b2"]


def kernel(**inputs):
    import concourse.bacc as bacc
    from concourse.bass_utils import run_bass_kernel_spmd

    nc = bacc.Bacc("TRN2", target_bir_lowering=False, num_devices=1)
    arrays, args = {}, []
    for name in _INS:
        a = np.ascontiguousarray(inputs[name])
        arrays[f"in_{name}"] = a
        args.append(nc.dram_tensor(f"in_{name}", a.shape, mybir.dt.from_np(a.dtype), kind="ExternalInput").ap())
    out = nc.dram_tensor("out", (BATCH, SEQ, MODEL), F32, kind="ExternalOutput").ap()
    program(nc, *args, out)
    r = run_bass_kernel_spmd(nc, [arrays], core_ids=[0])
    return r.results[0]["out"]
```

```python
from contextlib import ExitStack

import numpy as np

import concourse.bass as bass
from concourse import mybir

F32, F32R, BF16 = mybir.dt.float32, mybir.dt.float32r, mybir.dt.bfloat16
U32 = mybir.dt.uint32
ALU, ACT, AX = mybir.AluOpType, mybir.ActivationFunctionType, mybir.AxisListType

P = 128
BATCH, SEQ, MODEL = 8, 1024, 256
TOKENS = BATCH * SEQ
TILES = TOKENS // P
MC = MODEL // P
HEADS, HDIM = 16, 64
PAIRS = HEADS // 2
QT = SEQ // P
EXPERTS, TOPK, HIDDEN = 8, 2, 1024
CAP = TOPK * TOKENS // EXPERTS
SLOTS = EXPERTS * CAP
HC = HIDDEN // P
EPS = 1e-5
QSCALE = HDIM ** -0.5
MASKED = -0.7 * 3.3895314e38


class Count:

    def __init__(self, sem, per, start=0):
        self.sem, self.per, self.start = sem, per, start

    def wait(self, eng, n, k):
        eng.wait_ge(self.sem, n * self.per + (self.start + k))


def apart(eng, sem):
    eng.sem_inc(sem, 1)


def constants(nc, ctx):
    t = {}
    for name, dt in (("ident", F32), ("identb", BF16), ("mask", BF16), ("below", BF16), ("ones", BF16)):
        t[name] = ctx.enter_context(nc.sbuf_tensor(name, [P, P], dt))
    with ExitStack() as tmp:
        s_set, s_done = (tmp.enter_context(nc.semaphore(n)) for n in ("s_const_set", "s_const"))
        block = tmp.enter_context(nc.Block())

        @block.gpsimd
        def _(g):
            g.memset(t["ident"][:], 0.0)
            g.memset(t["identb"][:], 0.0)
            g.memset(t["mask"][:], 0.0)
            g.memset(t["ones"][:], 1.0)
            g.memset(t["below"][:], 0.0).then_inc(s_set, 1)
            g.wait_ge(s_set, 1)
            for name in ("ident", "identb"):
                g.affine_select(t[name][:], t[name][:], [[-1, P]], ALU.not_equal, 1.0, base=0, channel_multiplier=1)
            g.affine_select(t["mask"][:], t["mask"][:], [[-1, P]], ALU.is_ge, MASKED, base=0, channel_multiplier=1)
            g.affine_select(t["below"][:], t["below"][:], [[1, P]], ALU.is_gt, -1.0, base=0,
                            channel_multiplier=-1).then_inc(s_done, 1)
            g.wait_ge(s_done, 1)
    return t


def layernorm_and_router(nc, k, x, wg, xn_dram, logits):
    UT, RING = 4, 4
    UNITS = TILES // UT
    ROUNDS = UNITS // RING
    CU = RING // 2
    CT = CU * UT
    COLS = P // UT
    xv = x.rearrange("b s m -> (b s) m").rearrange("(u t p) m -> u p t m", t=UT, p=P)
    xnv = xn_dram.rearrange("(u t p) m -> u p t m", t=UT, p=P)
    with ExitStack() as c:
        sb = lambda n, s, d=F32: c.enter_context(nc.sbuf_tensor(n, s, d))
        ps = lambda n, s: c.enter_context(nc.psum_tensor(n, s, F32))
        sem = lambda n: c.enter_context(nc.semaphore(n))
        two = lambda f: [f(i) for i in range(2)]
        x4 = [sb(f"x4_{i}", [P, UT, MODEL]) for i in range(RING)]
        xn4 = [sb(f"xn4_{i}", [P, UT, MODEL]) for i in range(RING)]
        xT = two(lambda i: sb(f"xT_{i}", [P, UT * MC, P]))
        stats = two(lambda i: sb(f"stats_{i}", [P, CT, 6]))
        mv = two(lambda i: sb(f"mv_{i}", [P, CT, 2]))
        root = two(lambda i: sb(f"root_{i}", [P, CT]))
        guess, sq = sb("guess", [P, CT]), sb("sq", [P, CT])
        rstd = two(lambda i: sb(f"rstd_{i}", [P, CT]))
        wg_sb = sb("wg_sb", [P, MC, COLS])
        lT = two(lambda i: sb(f"lT_{i}", [P, P]))
        eps = sb("eps", [P, 1])
        pT = two(lambda i: ps(f"pT_{i}", [P, 2, 512]))
        pL = two(lambda i: ps(f"pL_{i}", [P, P]))
        pG = two(lambda i: ps(f"pG_{i}", [P, UT, COLS]))
        s_wg, s_wz, s_eps, s_apart = sem("s_wg"), sem("s_wz"), sem("s_eps"), sem("s_apart_ln")
        in_ = [Count(sem(f"s_in{i}"), 16) for i in range(RING)]
        out_ = [Count(sem(f"s_out{i}"), 16, 16) for i in range(RING)]
        stat = Count(sem("s_stat"), 1)
        norm = Count(sem("s_norm"), 1)
        normp = Count(sem("s_normp"), 1)
        tr = Count(sem("s_tr"), 1, RING)
        trc = Count(sem("s_trc"), 1)
        lg = Count(sem("s_lg"), 1)
        lgc = Count(sem("s_lgc"), 1)
        gt = Count(sem("s_gt"), 1)
        gtc = Count(sem("s_gtc"), 1)
        aggr = Count(sem("s_aggr"), 1)
        rooted = Count(sem("s_root"), 1)
        refine = Count(sem("s_refine"), 5)
        block = c.enter_context(nc.Block())

        DVE_TILES, POOL_TILES = range(UT - 1), range(UT - 1, UT)

        def normalise(e, q, tiles, done):
            h, at = q // CU, q % CU * UT
            for t in tiles:
                ins = e.tensor_scalar(xn4[q][:, t, :], x4[q][:, t, :], mv[h][:, at + t, 0:1],
                                      rstd[h][:, at + t:at + t + 1], ALU.subtract, ALU.mult)
            ins.then_inc(done.sem, 1)

        def rounds(eng, body, end):
            body(0, True, False)
            with eng.Fori(1, ROUNDS - 1 if end else ROUNDS) as i:
                body(i, False, False)
            if end:
                body(ROUNDS - 1, False, True)

        @block.sync
        def _(e):
            e.dma_start(x4[0][:], xv[0]).then_inc(in_[0].sem, 16)
            for q in range(RING):
                e.sem_inc(out_[q].sem, 16)
            e.wait_ge(s_wz, 1)
            e.dma_start(wg_sb[:, :, 0:EXPERTS], wg.rearrange("(c p) n -> p c n", p=P)).then_inc(s_wg, 16)
            for q in range(1, RING):
                e.dma_start(x4[q][:], xv[q]).then_inc(in_[q].sem, 16)

            def body(i, first, last):
                for q in range(RING):
                    u = i * RING + q
                    norm.wait(e, u, 1)
                    apart(e, s_apart)
                    normp.wait(e, u, 1)
                    apart(e, s_apart)
                    if not last:
                        e.dma_start(x4[q][:], xv[bass.ds(u + RING, 1)].rearrange("u p t m -> (u p) t m")).then_inc(in_[q].sem, 16)
                    e.dma_start(xnv[bass.ds(u, 1)].rearrange("u p t m -> (u p) t m"), xn4[q][:]).then_inc(out_[q].sem, 16)

            rounds(e, body, True)
            for q in range(RING):
                out_[q].wait(e, ROUNDS - 1, 16)

        @block.vector
        def _(e):
            e.memset(eps[:], EPS).then_inc(s_eps, 1)
            e.memset(wg_sb[:], 0.0).then_inc(s_wz, 1)

            def aggregate(u, q):
                h, at = q // CU, q % CU * UT
                stat.wait(e, u, 1)
                apart(e, s_apart)
                for t in range(at, at + UT):
                    ins = e.bn_aggr(mv[h][:, t, :], stats[h][:, t, :])
                if q % CU == CU - 1:
                    ins.then_inc(aggr.sem, 1)

            def invert(n, h):
                def step(ins, j):
                    ins.then_inc(refine.sem, 1)
                    if j < 5:
                        refine.wait(e, n, j)

                rooted.wait(e, n, 1)
                step(e.reciprocal(guess[:], root[h][:]), 1)
                step(e.tensor_tensor(sq[:], guess[:], guess[:], ALU.mult), 2)
                step(e.scalar_tensor_tensor(sq[:], mv[h][:, :, 1], EPS, sq[:], ALU.add, ALU.mult), 3)
                step(e.tensor_scalar(sq[:], sq[:], -0.5, 1.5, ALU.mult, ALU.add), 4)
                step(e.tensor_tensor(rstd[h][:], guess[:], sq[:], ALU.mult), 5)

            def finish(n, h, first):
                invert(n, h)
                refine.wait(e, n, 5)
                for b in range(CU):
                    q = h * CU + b
                    if not first:
                        out_[q].wait(e, (n - h) // 2 - 1, 16)
                        tr.wait(e, n * CU + b - RING, 1)
                    normalise(e, q, DVE_TILES, norm)

            def body(i, first, last):
                for q in range(RING):
                    u = i * RING + q
                    in_[q].wait(e, i, 16)
                    h, at = q // CU, q % CU * UT
                    for t in range(UT):
                        ins = e.bn_stats(stats[h][:, at + t, :], x4[q][:, t, :])
                    ins.then_inc(stat.sem, 1)
                    if q % CU == 0 and not (first and q == 0):
                        finish(2 * i + h - 1, 1 - h, first)
                    if q % CU == 0 and not first:
                        normp.wait(e, u - RING + CU - 1, 1)
                    aggregate(u, q)

            rounds(e, body, False)
            finish(2 * ROUNDS - 1, 1, False)

        @block.gpsimd
        def _(e):
            def body(i, first, last):
                for q in range(RING):
                    u = i * RING + q
                    refine.wait(e, 2 * i + q // CU, 5)
                    apart(e, s_apart)
                    if not first:
                        out_[q].wait(e, i - 1, 16)
                        apart(e, s_apart)
                        tr.wait(e, u - RING, 1)
                        apart(e, s_apart)
                    normalise(e, q, POOL_TILES, normp)

            rounds(e, body, False)

        @block.scalar
        def _(e):
            e.wait_ge(s_eps, 1)

            def sqrt(n, h):
                aggr.wait(e, n, 1)
                e.activation(root[h][:], mv[h][:, :, 1], ACT.Sqrt, bias=eps[:, 0:1]).then_inc(rooted.sem, 1)

            def take(u, b):
                lg.wait(e, u, 1)
                e.activation(lT[b][:], pL[b][:], ACT.Copy).then_inc(lgc.sem, 1)

            def keep(u, b):
                gt.wait(e, u, 1)
                apart(e, s_apart)
                e.activation(logits[:, bass.ds(u * UT, UT), :], pG[b][:, :, 0:EXPERTS], ACT.Copy).then_inc(gtc.sem, 1)

            def body(i, first, last):
                for q in range(RING):
                    u, b = i * RING + q, q % 2
                    if q % CU == 0 and not (last and q >= CU):
                        sqrt(2 * i + q // CU + 1, 1 - q // CU)
                    if not (first and q == 0):
                        take(u - 1, 1 - b)
                    tr.wait(e, u, 1)
                    for h in range(2):
                        ins = e.activation(xT[b][:, 4 * h:4 * h + 4, :].rearrange("p a b -> p (a b)"), pT[b][:, h, :], ACT.Copy)
                    ins.then_inc(trc.sem, 1)
                    if not (first and q == 0):
                        keep(u - 1, 1 - b)

            sqrt(0, 0)
            rounds(e, body, True)
            take(UNITS - 1, 1)
            keep(UNITS - 1, 1)

        @block.tensor
        def _(e):
            e.sem_inc(tr.sem, RING)
            e.wait_ge(s_wg, 16)

            def transposes(u, q, first):
                norm.wait(e, u, 1)
                normp.wait(e, u, 1)
                if not first:
                    trc.wait(e, u - 2, 1)
                for t in range(UT):
                    for m in range(MC):
                        n = t * MC + m
                        ins = e.transpose(pT[q % 2][:, n // 4, (n % 4) * P:(n % 4 + 1) * P],
                                          xn4[q][:, t, m * P:(m + 1) * P], k["ident"][:])
                ins.then_inc(tr.sem, 1)

            def product(u, b, first):
                trc.wait(e, u, 1)
                if not first:
                    lgc.wait(e, u - 2, 1)
                for m in range(MC):
                    for t in range(UT):
                        ins = e.matmul(pL[b][t * COLS:(t + 1) * COLS, :], wg_sb[:, m, :], xT[b][:, t * MC + m, :],
                                       start=(m == 0), stop=(m == MC - 1))
                ins.then_inc(lg.sem, 1)

            def turn(u, b, first):
                lgc.wait(e, u, 1)
                if not first:
                    gtc.wait(e, u - 2, 1)
                e.transpose(pG[b][:].rearrange("p t c -> p (t c)"), lT[b][:], k["ident"][:]).then_inc(gt.sem, 1)

            def body(i, first, last):
                for q in range(RING):
                    u = i * RING + q
                    if not (first and q == 0):
                        product(u - 1, (q + 1) % 2, first and q < 3)
                    transposes(u, q, first and q < 2)
                    if not (first and q == 0):
                        turn(u - 1, (q + 1) % 2, first and q < 3)

            rounds(e, body, False)
            product(UNITS - 1, 1, False)
            turn(UNITS - 1, 1, False)


def route(nc, k, logits, pick, slot_token, prefetch):
    E = EXPERTS
    SLOT_TILES = SLOTS // P
    with ExitStack() as c:
        sb = lambda n, s, d=F32: c.enter_context(nc.sbuf_tensor(n, s, d))
        sem = lambda n: c.enter_context(nc.semaphore(n))
        two = lambda f: [f(i) for i in range(2)]
        shape = [P, TILES, E]
        choices = [P, TOPK, TILES]
        ex, score, w, ramp = (sb(n, shape) for n in ("ex", "score", "w", "ramp"))
        hot = sb("hot", [P, TOPK, E, TILES], BF16)
        top = sb("top", choices)
        down = sb("down", choices)
        mx, tot, zeros = (sb(n, [P, TILES]) for n in ("mx", "tot", "zeros"))
        rank, run = (sb(n, [P, TOPK, E, TILES]) for n in ("rank", "run"))
        pos, val, col, high = (sb(n, choices) for n in ("pos", "val", "col", "high"))
        part = two(lambda i: sb(f"part{i}", choices, U32))
        token = sb("token", [P, TILES])
        GT = 2
        GROUPS, MARKS, RING = TILES // GT, GT * TOPK, 4
        column = sb("column", [P, MARKS, P])
        slot_low = sb("slot_low", [P, TILES, TOPK])
        slot_high = sb("slot_high", [P, TILES, TOPK])
        at_low = [sb(f"at_low{i}", [P, MARKS, P]) for i in range(RING)]
        at_high = [sb(f"at_high{i}", [P, MARKS, P]) for i in range(RING)]
        put = [sb(f"put{i}", [P, MARKS, P]) for i in range(RING)]
        pD, pN = (c.enter_context(nc.psum_tensor(n, [P, TOPK, E, TILES], F32)) for n in ("pD", "pN"))
        pS = c.enter_context(nc.psum_tensor("pS", [P, SLOT_TILES], F32))
        s_iota, s_chain, s_exp, s_hot, s_cnt, s_max = (
            sem(n) for n in ("s_iota", "s_chain", "s_exp", "s_hot", "s_cnt", "s_max"))
        s_apart = two(lambda i: sem(f"s_apart_route{i}"))
        low_ = Count(sem("s_low"), 1)
        high_ = Count(sem("s_high"), 1)
        put_ = Count(sem("s_put"), 1)
        added = Count(sem("s_added"), 1)
        block = c.enter_context(nc.Block())
        wide = lambda t: t.rearrange("p (t o) -> p t o", o=1).to_broadcast(shape)

        @block.sync
        def _(e):
            prefetch(e)

        @block.gpsimd
        def _(e):
            small = {"allow_small_or_imprecise_dtypes": True}
            e.iota(ramp[:], [[0, TILES], [-1, E]], base=E, channel_multiplier=0, **small).then_inc(s_iota, 1)
            e.iota(column[:], [[0, MARKS], [1, P]], base=0, channel_multiplier=0, **small)
            e.iota(token[:], [[P, TILES]], base=0, channel_multiplier=1, **small).then_inc(s_iota, 1)

        @block.vector
        def _(e):
            done = [0]

            def chain(ins):
                done[0] += 1
                ins.then_inc(s_chain, 1)
                e.wait_ge(s_chain, done[0])

            e.memset(zeros[:], 0.0)
            chain(e.tensor_reduce(mx[:], logits[:], AX.X, ALU.max))
            e.tensor_tensor(w[:], logits[:], wide(mx[:]), ALU.subtract).then_inc(s_max, 1)
            e.wait_ge(s_exp, 1)
            chain(e.tensor_reduce(tot[:], ex[:], AX.X, ALU.add))
            chain(e.reciprocal(mx[:], tot[:]))
            chain(e.tensor_tensor(score[:], ex[:], wide(mx[:]), ALU.mult))
            e.wait_ge(s_iota, 1)
            for j in range(TOPK):
                chain(e.tensor_reduce(top[:, j, :], score[:], AX.X, ALU.max))
                chain(e.tensor_tensor(w[:], score[:], wide(top[:, j, :]), ALU.is_equal))
                chain(e.tensor_tensor(w[:], w[:], ramp[:], ALU.mult))
                chain(e.tensor_reduce(down[:, j, :], w[:], AX.X, ALU.max))
                by_token = hot[:, j].rearrange("p e t -> p t e")
                e.tensor_tensor(by_token, w[:], wide(down[:, j, :]), ALU.is_equal).then_inc(s_hot, 1)
                if j == 0:
                    e.wait_ge(s_hot, 1)
                    chain(e.scalar_tensor_tensor(score[:], by_token, -4.0, score[:], ALU.mult, ALU.add))
            chain(e.tensor_tensor(tot[:], top[:, 0, :], top[:, 1, :], ALU.add))
            chain(e.reciprocal(mx[:], tot[:]))
            for j in range(TOPK):
                e.tensor_tensor(top[:, j, :], top[:, j, :], mx[:], ALU.mult)
            e.wait_ge(s_cnt, 1)
            for j in range(TOPK):
                for x in range(E):
                    init = 0.0 if j == 0 else run[:, 0, x, TILES - 1:TILES]
                    ins = e.tensor_tensor_scan(run[:, j, x, :], pN[:, j, x, :], zeros[:], init, ALU.add, ALU.add)
                chain(ins)
            chain(e.tensor_tensor(rank[:], run[:], pD[:], ALU.add))
            chain(e.tensor_tensor(rank[:], rank[:], hot[:], ALU.mult))
            chain(e.tensor_reduce(pos[:], rank[:].rearrange("p j e t -> p j t e"), AX.X, ALU.add))
            chain(e.tensor_scalar(val[:], pos[:], float(CAP), None, ALU.is_lt))
            chain(e.tensor_tensor(pos[:], pos[:], val[:], ALU.mult))
            chain(e.scalar_tensor_tensor(col[:], down[:], -float(CAP), pos[:], ALU.mult, ALU.add))
            row = pick[:, :, 0:TOPK].rearrange("p t j -> p j t")
            chain(e.tensor_scalar(row, col[:], float(E * CAP), None, ALU.add))
            e.tensor_tensor(pick[:, :, TOPK:].bitcast(F32).rearrange("p t j -> p j t"), top[:], val[:], ALU.mult)
            e.tensor_scalar(part[0][:], row, P - 1, None, ALU.bitwise_and)
            chain(e.tensor_scalar(part[1][:], row, P.bit_length() - 1, None, ALU.logical_shift_right))
            e.tensor_copy(slot_low[:].rearrange("p t j -> p j t"), part[0][:])
            chain(e.tensor_copy(high[:], part[1][:]))
            chain(e.scalar_tensor_tensor(high[:], high[:], 1.0, val[:], ALU.add, ALU.mult))
            chain(e.tensor_scalar(slot_high[:].rearrange("p t j -> p j t"), high[:], 1.0, None, ALU.subtract))

            def marks(i, first):
                for b in range(RING):
                    g = RING * i + b
                    if not first:
                        added.wait(e, g - RING, 1)
                        apart(e, s_apart[0])
                    for slot, at, written in ((slot_high, at_high, high_), (slot_low, at_low, low_)):
                        e.tensor_tensor(at[b][:], column[:], slot[:, bass.ds(g * GT, GT), :].rearrange("p t (j o) -> p (t j) o", o=1).to_broadcast([P, MARKS, P]),
                                        ALU.is_equal).then_inc(written.sem, 1)

            e.wait_ge(s_iota, 2)
            marks(0, True)
            with e.Fori(1, GROUPS // RING) as i:
                marks(i, False)
            added.wait(e, GROUPS - 1, 1)
            e.tensor_copy(slot_token[:], pS[:])

        @block.scalar
        def _(e):
            e.wait_ge(s_max, 1)
            e.activation(ex[:].rearrange("p a b -> p (a b)"), w[:].rearrange("p a b -> p (a b)"), ACT.Exp).then_inc(s_exp, 1)
            e.wait_ge(s_iota, 2)

            def puts(i, first):
                for b in range(RING):
                    g = RING * i + b
                    if not first:
                        added.wait(e, g - RING, 1)
                        apart(e, s_apart[1])
                    high_.wait(e, g, 1)
                    apart(e, s_apart[1])
                    for t in range(GT):
                        ms = slice(t * TOPK, (t + 1) * TOPK)
                        ins = e.activation(put[b][:, ms, :], at_high[b][:, ms, :], ACT.Copy,
                                           scale=token[:, bass.ds(g * GT + t, 1)])
                    ins.then_inc(put_.sem, 1)

            puts(0, True)
            with e.Fori(1, GROUPS // RING) as i:
                puts(i, False)

        @block.tensor
        def _(e):
            for j in range(TOPK):
                e.wait_ge(s_hot, j + 1)
                flat = lambda t: t[:, j].rearrange("p e t -> p (e t)")
                e.matmul(flat(pD), k["below"][:], flat(hot), start=True, stop=True)
                ins = e.matmul(flat(pN), k["ones"][:], flat(hot), start=True, stop=True)
            ins.then_inc(s_cnt, 1)

            def add(i, first, last):
                for b in range(RING):
                    g = RING * i + b
                    low_.wait(e, g, 1)
                    put_.wait(e, g, 1)
                    for m in range(MARKS):
                        ins = e.matmul(pS[:], at_low[b][:, m, :], put[b][:, m, :], start=(first and b == 0 and m == 0),
                                       stop=(last and b == RING - 1 and m == MARKS - 1))
                    ins.then_inc(added.sem, 1)

            add(0, True, False)
            with e.Fori(1, GROUPS // RING - 1) as i:
                add(i, False, False)
            add(GROUPS // RING - 1, False, True)


def weight_loads(nc, ctx, w1, b1, w2):
    sb = lambda n, s: ctx.enter_context(nc.sbuf_tensor(n, s, F32))
    t = {"w1r": sb("w1r", [P, MC, HIDDEN]), "w2r": sb("w2r", [P, HC, MODEL]), "b1r": sb("b1r", [EXPERTS * HC, P]),
         "s_wload": ctx.enter_context(nc.semaphore("s_wload")), "s_b1": ctx.enter_context(nc.semaphore("s_b1"))}

    def first(e):
        e.dma_start(t["w1r"][:], w1[0].rearrange("(c p) h -> p c h", p=P)).then_inc(t["s_wload"], 16)
        e.dma_start(t["w2r"][:], w2[0].rearrange("(c p) m -> p c m", p=P)).then_inc(t["s_wload"], 16)
        e.dma_start(t["b1r"][:], b1.rearrange("e (h p) -> (e h) p", p=P)).then_inc(t["s_b1"], 16)

    return t, first


def experts(nc, k, xn_dram, slot_token, raw, w1, w2, b2, y_dram):
    GS = 512
    GROUPS = SLOTS // GS
    PER = CAP // GS
    GT = GS // P
    with ExitStack() as c:
        sb = lambda n, s, d=F32: c.enter_context(nc.sbuf_tensor(n, s, d))
        ps = lambda n, s: c.enter_context(nc.psum_tensor(n, s, F32))
        sem = lambda n: c.enter_context(nc.semaphore(n))
        two = lambda f: [f(i) for i in range(2)]
        idx = two(lambda i: sb(f"idx{i}", [P, GT], U32))
        xg = two(lambda i: sb(f"xg{i}", [P, GT, MODEL]))
        xh = two(lambda i: sb(f"xh{i}", [P, MC, GS], F32R))
        xl = two(lambda i: sb(f"xl{i}", [P, MC, GS], F32R))
        w1r, w2r, b1r, s_b1 = raw["w1r"], raw["w2r"], raw["b1r"], raw["s_b1"]
        w1h, w1l = (two(lambda i: sb(f"w1{n}{i}", [P, MC, HIDDEN], F32R)) for n in "hl")
        w2h, w2l = (two(lambda i: sb(f"w2{n}{i}", [P, HC, MODEL], F32R)) for n in "hl")
        b1T = sb("b1T", [P, EXPERTS * HC])
        b1c = two(lambda i: sb(f"b1c{i}", [P, HC]))
        b2c = two(lambda i: sb(f"b2c{i}", [P, MODEL]))
        h32 = two(lambda i: sb(f"h32_{i}", [P, GS]))
        hh = two(lambda i: sb(f"hh{i}", [P, HC, GS], F32R))
        hl = two(lambda i: sb(f"hl{i}", [P, HC, GS], F32R))
        yb = [sb(f"yb{i}", [P, MODEL]) for i in range(GT)]
        pX = two(lambda i: ps(f"pX{i}", [P, GS]))
        pH = [ps(f"pH{i}", [P, GS]) for i in range(4)]
        pY = two(lambda i: ps(f"pY{i}", [P, MODEL]))
        s_b1t, s_b1c0 = sem("s_b1t"), sem("s_b1c0")
        s_apart = two(lambda i: sem(f"s_apart_ffn{i}"))
        wload = Count(raw["s_wload"], 48)
        whi = Count(sem("s_whi"), 2)
        wlo = Count(sem("s_wlo"), 2)
        bias = Count(sem("s_bias"), 1)
        staged = Count(sem("s_staged"), 1)
        gat = two(lambda i: Count(sem(f"s_gat{i}"), 16 * GT))
        tX = Count(sem("s_tX"), 1)
        xhi, xlo = Count(sem("s_xhi"), 1), Count(sem("s_xlo"), 1)
        fH = Count(sem("s_fH"), HC)
        rl = Count(sem("s_rl"), HC)
        hhi = Count(sem("s_hhi"), HC)
        hlo = Count(sem("s_hlo"), HC)
        fY = Count(sem("s_fY"), GT)
        yv = Count(sem("s_yv"), GT)
        yst = [Count(sem(f"s_yst{i}"), 16) for i in range(GT)]
        block = c.enter_context(nc.Block())
        NE = EXPERTS // 2
        row = lambda v, e: v[bass.ds(e, 1)]

        def loop(eng, body):
            body(0, True, False)
            with eng.Fori(1, NE - 1) as i:
                body(i, False, False)
            body(NE - 1, False, True)

        w1v = w1.rearrange("e (c p) h -> e p c h", p=P)
        w2v = w2.rearrange("e (c p) m -> e p c m", p=P)
        yv_d = y_dram.rearrange("(s p) m -> s p m", p=P)

        @block.sync
        def _(e):
            def load_w(x, q):
                e.dma_start(w1r[:], row(w1v, x).rearrange("e p c h -> (e p) c h")).then_inc(wload.sem, 16)
                e.dma_start(w2r[:], row(w2v, x).rearrange("e p c h -> (e p) c h")).then_inc(wload.sem, 16)
                e.dma_start(b2c[q][:], row(b2, x).to_broadcast([P, MODEL])).then_inc(wload.sem, 16)

            e.dma_start(b2c[0][:], b2[0:1].to_broadcast([P, MODEL])).then_inc(wload.sem, 16)

            def body(i, first, last):
                for par in range(2):
                    x = 2 * i + par
                    for g in range(PER):
                        sg, q = PER * x + g, g % 2
                        if g == 0 and not (last and par == 1):
                            wlo.wait(e, x, 2)
                            if not (first and par == 0):
                                apart(e, s_apart[1])
                                yv.wait(e, sg, 0)
                            apart(e, s_apart[1])
                            load_w(x + 1, 1 - par)
                        for t in range(GT):
                            if first and par == 0 and g == 0:
                                continue
                            yv.wait(e, sg - 1, t + 1)
                            apart(e, s_apart[1])
                            e.dma_start(row(yv_d, (sg - 1) * GT + t).rearrange("s p m -> (s p) m"), yb[t][:]).then_inc(yst[t].sem, 16)

            loop(e, body)
            for t in range(GT):
                yv.wait(e, GROUPS - 1, t + 1)
                e.dma_start(yv_d[(GROUPS - 1) * GT + t], yb[t][:]).then_inc(yst[t].sem, 16)
            for t in range(GT):
                yst[t].wait(e, GROUPS - 1, 16)

        @block.gpsimd
        def _(e):
            def gather(sg, half, q, first=False):
                if not first:
                    gat[q].wait(e, half - 1, 16 * GT)
                    apart(e, s_apart[0])
                    tX.wait(e, sg - 2, 1)
                    apart(e, s_apart[0])
                e.tensor_copy(idx[q][:], slot_token[:, bass.ds(sg * GT, GT)]).then_inc(staged.sem, 1)
                staged.wait(e, sg, 1)
                apart(e, s_apart[0])
                for t in range(GT):
                    e.indirect_dma_start(xg[q][:, t, :], None, xn_dram,
                                         bass.IndirectOffsetOnAxis(ap=idx[q][:, t:t + 1], axis=0)).then_inc(gat[q].sem, 16)

            def split(x, q):
                wload.wait(e, x, 48)
                apart(e, s_apart[0])
                for raw, hi in ((w1r, w1h[q]), (w2r, w2h[q])):
                    e.tensor_scalar(hi[:].rearrange("p a b -> p (a b)"), raw[:].rearrange("p a b -> p (a b)"), 1.0, 1.0,
                                    ALU.mult, ALU.mult).then_inc(whi.sem, 1)

            gather(0, 0, 0, True)
            split(0, 0)
            gather(1, 0, 1, True)

            def body(i, first, last):
                for par in range(2):
                    x = 2 * i + par
                    for g in range(PER):
                        sg = PER * x + g
                        if not (last and par == 1 and g >= PER - 2):
                            gather(sg + 2, i * PER + (par * PER + g) // 2 + 1, g % 2)
                        if g == 1 and not (last and par == 1):
                            fY.wait(e, sg - 1, 0)
                            split(x + 1, 1 - par)

            loop(e, body)

        @block.tensor
        def _(e):
            def rows(sg, half, q, first=False):
                gat[q].wait(e, half, 16 * GT)
                if not first:
                    xhi.wait(e, sg - 1, 1)
                    xlo.wait(e, sg - 1, 1)
                for m in range(MC):
                    for t in range(GT):
                        ins = e.transpose(pX[m][:, t * P:(t + 1) * P], xg[q][:, t, m * P:(m + 1) * P], k["ident"][:])
                ins.then_inc(tX.sem, 1)

            def up(sg, par, q, hc, first):
                if hc == 0:
                    xhi.wait(e, sg, 1)
                    xlo.wait(e, sg, 1)
                if not (first and hc < 4):
                    rl.wait(e, sg, hc - 3)
                ws = slice(hc * P, (hc + 1) * P)
                terms = [(w1h, xh), (w1h, xl), (w1l, xh)]
                n = 0
                for m in range(MC):
                    for w, xx in terms:
                        ins = e.matmul(pH[hc % 4][:], w[par][:, m, ws], xx[q][:, m, :], start=(n == 0), stop=(n == 3 * MC - 1))
                        n += 1
                ins.then_inc(fH.sem, 1)

            def down(sg, par, q, t, first):
                if t == 0:
                    hlo.wait(e, sg, HC)
                if not (first and t < 2):
                    yv.wait(e, sg, t - 1)
                ts_ = slice(t * P, (t + 1) * P)
                for hc in range(HC):
                    for n, (hs, ws) in enumerate(((hh, w2h), (hh, w2l), (hl, w2h))):
                        ins = e.matmul(pY[t % 2][:], hs[q][:, hc, ts_], ws[par][:, hc, :],
                                       start=(hc == 0 and n == 0), stop=(hc == HC - 1 and n == 2))
                ins.then_inc(fY.sem, 1)

            e.wait_ge(s_b1, 16)
            e.transpose(pY[0][:, 0:EXPERTS * HC], b1r[:], k["ident"][0:EXPERTS * HC, 0:EXPERTS * HC]).then_inc(s_b1t, 1)
            rows(0, 0, 0, True)
            e.wait_ge(s_b1c0, 1)

            def body(i, first, last):
                for par in range(2):
                    x = 2 * i + par
                    for g in range(PER):
                        sg = PER * x + g
                        start = first and par == 0 and g == 0
                        for hc in range(HC):
                            if g == 0 and hc == 0:
                                wlo.wait(e, x, 1)
                            up(sg, par, g % 2, hc, start)
                            if hc == 2 and not (last and par == 1 and g == PER - 1):
                                rows(sg + 1, i * PER + (par * PER + g + 1) // 2, (g + 1) % 2)
                            if g == 1 and hc == 1:
                                wlo.wait(e, x, 2)
                            if hc % 2 and not start:
                                down(sg - 1, par if g else 1 - par, (g + 1) % 2, hc // 2,
                                     first and par == 0 and g == 1)

            loop(e, body)
            for t in range(GT):
                down(GROUPS - 1, 1, 1, t, False)

        @block.scalar
        def _(e):
            def rows(sg, q, first=False):
                tX.wait(e, sg, 1)
                if not first:
                    fH.wait(e, sg - 2, HC)
                for m in range(MC):
                    ins = e.activation(xh[q][:, m, :], pX[m][:], ACT.Copy)
                ins.then_inc(xhi.sem, 1)

            e.wait_ge(s_b1t, 1)
            e.activation(b1T[:], pY[0][:, 0:EXPERTS * HC], ACT.Copy).then_inc(s_b1c0, 1)
            rows(0, 0, True)

            def body(i, first, last):
                for par in range(2):
                    x = 2 * i + par
                    e.wait_ge(s_b1c0, 1)
                    e.activation(b1c[par][:], b1T[:, bass.ds(x * HC, HC)], ACT.Copy).then_inc(bias.sem, 1)
                    bias.wait(e, x, 1)
                    for g in range(PER):
                        sg, q = PER * x + g, g % 2
                        start = first and par == 0 and g == 0
                        for hc in range(HC):
                            fH.wait(e, sg, hc + 1)
                            if not (start and hc < 2):
                                hlo.wait(e, sg, hc - 1)
                            e.activation(h32[hc % 2][:], pH[hc % 4][:], ACT.Relu, bias=b1c[par][:, hc:hc + 1]).then_inc(rl.sem, 1)
                            rl.wait(e, sg, hc + 1)
                            if hc == 0 and not (first and par == 0 and g < 2):
                                fY.wait(e, sg - 2, GT)
                            e.activation(hh[q][:, hc, :], h32[hc % 2][:], ACT.Copy).then_inc(hhi.sem, 1)
                            if hc == 2 and not (last and par == 1 and g == PER - 1):
                                rows(sg + 1, (g + 1) % 2, start)

            loop(e, body)

        @block.vector
        def _(e):
            def rows(sg, q):
                xhi.wait(e, sg, 1)
                for m in range(MC):
                    ins = e.tensor_tensor(xl[q][:, m, :], pX[m][:], xh[q][:, m, :].bitcast(F32), ALU.subtract)
                ins.then_inc(xlo.sem, 1)

            def split(x, q, j):
                raw, hi, lo = ((w1r, w1h[q], w1l[q]), (w2r, w2h[q], w2l[q]))[j]
                whi.wait(e, x, j + 1)
                e.tensor_tensor(lo[:], raw[:], hi[:].bitcast(F32), ALU.subtract).then_inc(wlo.sem, 1)

            def down(sg, par, t, first):
                fY.wait(e, sg, t + 1)
                if not first:
                    yst[t].wait(e, sg - 1, 16)
                e.tensor_tensor(yb[t][:], pY[t % 2][:], b2c[par][:], ALU.add).then_inc(yv.sem, 1)

            split(0, 0, 0)
            rows(0, 0)
            split(0, 0, 1)

            def body(i, first, last):
                for par in range(2):
                    x = 2 * i + par
                    for g in range(PER):
                        sg, q = PER * x + g, g % 2
                        start = first and par == 0 and g == 0
                        for hc in range(HC):
                            hhi.wait(e, sg, hc + 1)
                            e.tensor_tensor(hl[q][:, hc, :], h32[hc % 2][:], hh[q][:, hc, :].bitcast(F32),
                                            ALU.subtract).then_inc(hlo.sem, 1)
                            if hc == 2 and not (last and par == 1 and g == PER - 1):
                                rows(sg + 1, (g + 1) % 2)
                            if hc % 2 and not start:
                                down(sg - 1, par if g else 1 - par, hc // 2, first and par == 0 and g == 1)
                            if g == 2 and hc in (4, 6) and not (last and par == 1):
                                split(x + 1, 1 - par, hc // 2 - 2)

            loop(e, body)
            for t in range(GT):
                down(GROUPS - 1, 1, t, False)


def attention_and_sum(nc, k, x, xn_dram, w_qkv, w_out, pick, y_dram, out):
    UNITS = BATCH * PAIRS
    STEPS, LAG, RING = 2 * QT, 3, 4
    HALF = 512
    HT = HALF // P
    GQ = 2 * P
    GROUPS = SEQ // GQ
    PART = 4
    PARTS = [-(-(2 * g + 2) // PART) for g in range(GROUPS)]
    AHEAD = QT + 1
    width = lambda s: (s // 2 + 1) * P
    shift = lambda s: P if width(s) == HALF + P else 0
    CH = [[b for b in (min(HT, s // 2 + 1), s // 2 + 1 - HT) if b > 0] for s in range(STEPS)]
    FIRST_CH = [sum(len(x) for x in CH[:s]) for s in range(STEPS + 1)]
    CHUNKS = FIRST_CH[STEPS]
    assert all(FIRST_CH[4 * g] % 2 == 0 for g in range(GROUPS + 1)) and STEPS % RING == 0

    STEP_OF = {"q0": 0, "q1": 1, "k0": 1, "k1": 2, "v0": 3, "xn": 4, "t0": 6, "v1": 8, "o0": 7, "t1": 9, "o1": 10,
               "o2": 12, "o3": 13}
    FULL = sorted(STEP_OF, key=STEP_OF.get)
    BEFORE = [p for p in FULL if p[0] in "qkvt"]
    FIRST = [p for p in FULL if p[0] != "o"]
    TAIL = [p for p in FULL if p[0] == "o"]
    SHORT = 2 * HT
    BANK_OF = {p: i % 3 if STEP_OF[p] < SHORT else 2 for i, p in enumerate(FULL)}
    assert all(STEP_OF[p] >= 1 for p in FULL if BANK_OF[p] == 1)
    BY_ACT = {"q0", "q1", "k0", "k1", "v0", "v1", "xn"}
    BY_DVE = {"q0", "q1", "k0", "k1", "t0", "t1", "xn", "o0", "o1", "o2", "o3"}

    def pieces(n):
        if isinstance(n, int):
            return BEFORE if n < 0 else FIRST if n == 0 else TAIL if n >= UNITS - 1 else FULL
        return FULL

    class Pieces:

        def __init__(self, sem_, own):
            self.sem, self.own = sem_, own
            self.of = lambda names: sum(x in own for x in names)

        def wait(self, eng, n, name=None):
            if isinstance(n, int):
                v = sum(self.of(pieces(m)) for m in range(-1, n))
            else:
                v = n * self.of(FULL) + (self.of(BEFORE) + self.of(FIRST) - self.of(FULL))
            if name is not None:
                names = pieces(n)
                v = v + self.of(names[:names.index(name) + 1])
            eng.wait_ge(self.sem, v)

    with ExitStack() as c:
        sb = lambda n, s, d=F32: c.enter_context(nc.sbuf_tensor(n, s, d))
        ps = lambda n, s: c.enter_context(nc.psum_tensor(n, s, F32))
        sem = lambda n: c.enter_context(nc.semaphore(n))
        two = lambda f: [f(i) for i in range(2)]
        qh, ql = (two(lambda i: two(lambda h: sb(f"q{n}{i}{h}", [P, SEQ], F32R))) for n in "hl")
        kk = two(lambda i: two(lambda h: sb(f"kk{i}{h}", [P, SEQ], F32R)))
        vv = two(lambda i: sb(f"vv{i}", [P, QT, P]))
        vT = sb("vT", [P, HALF])
        pT = two(lambda h: two(lambda g: sb(f"pT{h}{g}", [P, QT - 2 + 2 * g, GQ])))
        pr = [sb(f"pr{i}", [P, SEQ]) for i in range(RING)]
        negm, rsum, rinv = (sb(n, [P, RING]) for n in ("negm", "rsum", "rinv"))
        oh, ol = (two(lambda i: sb(f"o{n}{i}", [P, SEQ], F32R)) for n in "hl")
        xnh, xnl = (sb(f"xn{n}", [P, 2 * QT, MC, P], F32R) for n in "hl")
        xnt = sb("xnt", [P, MODEL])
        wr = sb("wr", [P, MC, 2, 3 * HDIM])
        wh, wl = (sb(f"w{n}", [P, MC, 3, 2, HDIM], F32R) for n in "hl")
        woh, wol = (sb(f"wo{n}", [P, PAIRS, MODEL], F32R) for n in "hl")
        res = sb("res", [P, 2 * QT, MODEL])
        yg = two(lambda j: sb(f"yg{j}", [P, MODEL]))
        sel = sb("sel", [P, 4], U32)
        ot = two(lambda i: sb(f"ot{i}", [P, MODEL]))
        S = two(lambda i: ps(f"S{i}", [P, SEQ]))
        T = two(lambda i: ps(f"T{i}", [P, HALF]))
        O = ps("O", [P, GQ])
        W0 = ps("W", [P, HALF])
        banks = [S[0][:, HALF:], S[1][:, HALF:], W0[:]]
        work_bank = lambda name: banks[BANK_OF[name]]

        row = lambda v, i: v[bass.ds(i, 1)]
        flat = lambda t: t.rearrange("p a b -> p (a b)")

        def split_weights(e, s_hi, wait_hi, s_lo):
            raw = lambda m: wr[:, m].rearrange("p h (w d) -> p h w d", d=HDIM)
            put = lambda t, m: t[:, m].rearrange("p w h d -> p h w d")
            for m in range(MC):
                ins = e.tensor_scalar(put(wh, m), raw(m), 1.0, 1.0, ALU.mult, ALU.mult)
            ins.then_inc(s_hi, 1)
            wait_hi()
            for m in range(MC):
                ins = e.tensor_tensor(put(wl, m), raw(m), put(wh, m).bitcast(F32), ALU.subtract)
            ins.then_inc(s_lo, 1)

        xv = x.rearrange("b (t p) m -> (b t) p m", p=P)
        outv = out.rearrange("b (t p) m -> (b t) p m", p=P)
        xnv = xn_dram.rearrange("(t p) m -> t p m", p=P)
        wv = w_qkv.rearrange("(c p) (g h) d -> g p c (h d)", p=P, h=2)
        wov = w_out.rearrange("(g h) d m -> (h d) g m", h=2)

        with ExitStack() as pre:
            psem = lambda n: pre.enter_context(nc.semaphore(n))
            s_wo, s_wohi, s_wolo, s_res0, s_w0, s_w0hi, s_w0lo = (
                psem(n) for n in ("s_wo", "s_wohi", "s_wolo", "s_res0", "s_w0", "s_w0hi", "s_w0lo"))
            CT = SEQ // MODEL
            loads = range(-(-AHEAD // CT))
            s_xn = [psem(f"s_xn{i}") for i in loads]
            s_tr, s_hi, s_lo = (psem(n) for n in ("s_ptr", "s_phi", "s_plo"))
            wo_raw = res[:, QT:2 * QT, :]
            raw_xn = [pr[t // CT][:, t % CT * MODEL:(t % CT + 1) * MODEL] for t in range(AHEAD)]
            bank = [T[0], T[1], W0, S[0]]
            block = pre.enter_context(nc.Block())

            @block.sync
            def _(e):
                e.dma_start(wr[:].rearrange("p c h d -> p c (h d)"), wv[0]).then_inc(s_w0, 16)
                for i in loads:
                    n = min(CT, AHEAD - CT * i)
                    e.dma_start(pr[i][:, 0:n * MODEL].rearrange("p (t m) -> p t m", m=MODEL),
                                xnv[CT * i:CT * i + n].rearrange("t p m -> p t m")).then_inc(s_xn[i], 16)
                e.dma_start(wo_raw, wov).then_inc(s_wo, 16)
                e.dma_start(res[:, 0:QT, :], x[0].rearrange("(t p) m -> p t m", p=P)).then_inc(s_res0, 16)
                e.wait_ge(s_res0, 16)

            @block.tensor
            def _(e):
                for t in range(AHEAD):
                    e.wait_ge(s_xn[t // CT], 16)
                    if t >= 4:
                        e.wait_ge(s_lo, t - 3)
                    for m in range(MC):
                        ins = e.transpose(bank[t % 4][:, m * P:(m + 1) * P], raw_xn[t][:, m * P:(m + 1) * P], k["ident"][:])
                    ins.then_inc(s_tr, 1)

            @block.scalar
            def _(e):
                for t in range(AHEAD):
                    e.wait_ge(s_tr, t + 1)
                    e.activation(flat(xnh[:, t]), bank[t % 4][:, 0:MODEL], ACT.Copy).then_inc(s_hi, 1)

            @block.vector
            def _(e):
                for t in range(AHEAD):
                    e.wait_ge(s_hi, t + 1)
                    e.tensor_tensor(flat(xnl[:, t]), bank[t % 4][:, 0:MODEL], flat(xnh[:, t]).bitcast(F32),
                                    ALU.subtract).then_inc(s_lo, 1)
                e.wait_ge(s_wohi, 1)
                e.tensor_tensor(wol[:], wo_raw, woh[:].bitcast(F32), ALU.subtract).then_inc(s_wolo, 1)

            @block.gpsimd
            def _(e):
                e.wait_ge(s_w0, 16)
                split_weights(e, s_w0hi, lambda: e.wait_ge(s_w0hi, 1), s_w0lo)
                e.wait_ge(s_wo, 16)
                e.tensor_scalar(woh[:], wo_raw, 1.0, 1.0, ALU.mult, ALU.mult).then_inc(s_wohi, 1)

        score = Count(sem("s_score"), STEPS)
        negmax = Count(sem("s_negmax"), STEPS)
        expd = Count(sem("s_expd"), STEPS)
        recip = Count(sem("s_recip"), STEPS)
        scaled = Count(sem("s_scaled"), STEPS)
        turned = Count(sem("s_turned"), CHUNKS)
        kept = two(lambda i: Count(sem(f"s_kept{i}"), CHUNKS // 2))
        pv = Count(sem("s_pv"), GROUPS)
        ohi, olo = Count(sem("s_ohi"), GROUPS), Count(sem("s_olo"), GROUPS)
        filled = Pieces(sem("s_filled"), set(FULL))
        act = Pieces(sem("s_act"), BY_ACT)
        dve = Pieces(sem("s_dve"), BY_DVE)
        dup = Count(sem("s_dup"), 64)
        wload = Count(sem("s_wload_a"), 16)
        whi, wlo = Count(sem("s_whi_a"), 1), Count(sem("s_wlo_a"), 1)
        xload = Count(sem("s_xload"), 16)
        rload = Count(sem("s_rload"), 16)
        picked = Count(sem("s_picked"), 1)
        ygot = Count(sem("s_ygot"), 32)
        sum1, sum2 = (Count(sem(f"s_sum{i}"), 1) for i in range(2))
        summed = Count(sem("s_summed"), 1, 1)
        stored = two(lambda i: Count(sem(f"s_stored{i}"), 16, 16))
        s_apart = {n: sem(f"s_apart_{n}") for n in ("sp", "pool", "act")}
        s_last_y = sem("s_last_y")
        s_last_sum = sem("s_last_sum")
        s_last_out = sem("s_last_out")
        block = c.enter_context(nc.Block())

        def units(eng, unit):
            def pair(j, early, first=False, last=False):
                for q in range(2):
                    unit(2 * j + q, q, j, early, first and q == 0, last and q == 1)

            pair(0, True, first=True)
            with eng.Fori(1, QT // 2) as j:
                pair(j, True)
            with eng.Fori(QT // 2, UNITS // 2 - 1) as j:
                pair(j, False)
            pair(UNITS // 2 - 1, False, last=True)

        def lagged(n, q, s):
            return (n, q, s - LAG) if s >= LAG else (n - 1, 1 - q, s - LAG + STEPS)

        def group_at(n, q, s):
            for d in range(2):
                for g in range(GROUPS):
                    part = s + d * STEPS - (4 * g + 3 + LAG + 1)
                    if 0 <= part < PARTS[g]:
                        return (n - d, (q + d) % 2, g, part)
            return None

        LAST = TILES - QT
        spare = [t[0][h][:, i * MODEL:(i + 1) * MODEL].bitcast(F32) for t in (qh, ql) for h in range(2) for i in range(SEQ // MODEL)]
        last_y = [spare[j * QT:(j + 1) * QT] for j in range(TOPK)]
        real = lambda n: not (isinstance(n, int) and n < 0)
        exists = lambda n: not (isinstance(n, int) and not 0 <= n < UNITS)

        @block.sync
        def _(e):
            def load_w(n):
                e.dma_start(wr[:].rearrange("p c h d -> p c (h d)"),
                            row(wv, n % PAIRS).rearrange("g p c d -> (g p) c d")).then_inc(wload.sem, 16)

            def double(n, q):
                act.wait(e, n, "q1")
                apart(e, s_apart["sp"])
                dve.wait(e, n, "q1")
                apart(e, s_apart["sp"])
                for t in (qh, ql):
                    e.dma_start(t[q][0][HDIM:P, :].bitcast(F32), t[q][0][0:HDIM, :].bitcast(F32)).then_inc(dup.sem, 16)
                    e.dma_start(t[q][1][0:HDIM, :].bitcast(F32), t[q][1][HDIM:P, :].bitcast(F32)).then_inc(dup.sem, 16)

            for t in stored:
                e.sem_inc(t.sem, 16)
            load_w(1)
            double(-1, 0)
            wlo.wait(e, 0, 1)
            load_w(2)

            def unit(n, q, j, early, first, last):
                if not last:
                    if not first:
                        filled.wait(e, n - 1, "xn")
                        apart(e, s_apart["sp"])
                    e.dma_start(xnt[:], row(xnv, (n + AHEAD) % TILES).rearrange("t p m -> (t p) m")).then_inc(xload.sem, 16)
                    double(n, 1 - q)
                    if not (isinstance(n, int) and n > 1):
                        wlo.wait(e, n + 1, 1)
                        apart(e, s_apart["sp"])
                        load_w(n + 3)
                if not early:
                    summed.wait(e, n - QT, 1)
                    apart(e, s_apart["sp"])
                    e.dma_start(row(outv, n - QT).rearrange("t p m -> (t p) m"), ot[q][:]).then_inc(stored[q].sem, 16)
                if not (isinstance(n, int) and n > 1):
                    e.dma_start(flat(res[:, bass.ds((n + QT) % (2 * QT), 1), :]),
                                row(xv, (n + QT) % TILES).rearrange("t p m -> (t p) m")).then_inc(rload.sem, 16)

            units(e, unit)
            for j in range(QT // 2):
                dve.wait(e, UNITS, f"o{j}")
                for t in (2 * j, 2 * j + 1):
                    e.dma_start(outv[LAST + t], res[:, (LAST + t) % (2 * QT), :]).then_inc(s_last_out, 16)
            for q in range(2):
                stored[q].wait(e, LAST // 2 - 1, 16)
            e.wait_ge(s_last_out, 16 * QT)

        @block.tensor
        def _(e):
            def project(n, name):
                W = work_bank(name)
                w, f = "qkv".index(name[0]), int(name[1])
                if name == "q0" and real(n):
                    wlo.wait(e, n, 1)
                i = 0
                t0 = ((n + 1) // PAIRS) % 2 * QT + f * HT
                for m in range(MC):
                    for ws, xs in ((wh, xnh), (wh, xnl), (wl, xnh)):
                        ins = e.matmul(W, ws[:, m, w].rearrange("p h d -> p (h d)"), xs[:, bass.ds(t0, HT), m, :],
                                       start=(i == 0), stop=(i == 3 * MC - 1))
                        i += 1
                return ins

            def turn_v(name):
                W = work_bank(name)
                for b in range(HT):
                    ins = e.transpose(W[:, b * P:(b + 1) * P], vT[:, b * P:(b + 1) * P], k["ident"][:])
                return ins

            def turn_xn(n):
                xload.wait(e, n, 16)
                W = work_bank("xn")
                for m in range(MC):
                    ins = e.transpose(W[:, m * P:(m + 1) * P], xnt[:, m * P:(m + 1) * P], k["ident"][:])
                return ins

            def out_project(n, q, j):
                W = work_bank(f"o{j}")
                if j == 0:
                    olo.wait(e, n, GROUPS)
                for t in range(2):
                    ts_ = slice((2 * j + t) * P, (2 * j + t + 1) * P)
                    for i, (os_, ws) in enumerate(((oh, woh), (oh, wol), (ol, woh))):
                        ins = e.matmul(W[:, t * MODEL:(t + 1) * MODEL], os_[q][:, ts_],
                                       flat(ws[:, bass.ds(n % PAIRS, 1), :]), start=(i == 0), stop=(i == 2))
                return ins

            def work(n, q, name):
                before = pieces(n)[:pieces(n).index(name)]
                same = [x for x in before if BANK_OF[x] == BANK_OF[name]]
                prev = same[-1] if same else None
                if prev is not None or (BANK_OF[name] == 2 and real(n)) or (isinstance(n, int) and n == 0):
                    if prev is None or prev in BY_ACT:
                        act.wait(e, n, prev)
                    if prev is None or prev in BY_DVE:
                        dve.wait(e, n, prev)
                if name == "t0" or name == "t1":
                    act.wait(e, n, "v" + name[1])
                if name[0] in "qkv":
                    ins = project(n, name)
                elif name[0] == "t":
                    ins = turn_v(name)
                elif name == "xn":
                    ins = turn_xn(n)
                else:
                    ins = out_project(n - 1, 1 - q, int(name[1]))
                ins.then_inc(filled.sem, 1)

            def scores(n, q, s, first):
                i, h = s // 2, s % 2
                if s == 0:
                    dup.wait(e, n, 64)
                    act.wait(e, n - 1, "k1")
                    dve.wait(e, n - 1, "k1")
                if not (first and s < 2):
                    expd.wait(e, n, s - 1)
                if s in (SHORT, SHORT + 1):
                    there = [x for x in pieces(n) if BANK_OF[x] == s % 2]
                    for own, count in ((BY_ACT, act), (BY_DVE, dve)):
                        mine = [x for x in there if x in own]
                        if mine:
                            count.wait(e, n, mine[-1])
                off, w = shift(s), max(width(s), 2 * P)
                cuts = [off] + [b for b in (HALF,) if off < b < off + w] + [off + w]
                for a, b in zip(cuts, cuts[1:]):
                    diag = off + i * P
                    here = a <= diag < b
                    for t in (qh, ql):
                        ins = e.matmul(S[s % 2][:, a:b], t[q][h][:, i * P:(i + 1) * P], kk[q][h][:, a - off:b - off],
                                       start=(t is qh), stop=(t is ql and not here))
                    if here:
                        ins = e.matmul(S[s % 2][:, diag:diag + P], k["identb"][:], k["mask"][:], start=False, stop=True)
                ins.then_inc(score.sem, 1)

            def turn_p(n, q, s):
                scaled.wait(e, n, s + 1)
                for i, blocks in enumerate(CH[s]):
                    ch = FIRST_CH[s] + i
                    if not (isinstance(n, int) and n == 0 and ch < 2):
                        kept[ch % 2].wait(e, n, ch // 2)
                    for b in range(blocks):
                        kt = i * HT + b
                        ins = e.transpose(T[ch % 2][:, b * P:(b + 1) * P], pr[s % RING][:, kt * P:(kt + 1) * P], k["ident"][:])
                    ins.then_inc(turned.sem, 1)

            def values(n, q, g, part):
                if part == 0:
                    for i in range(2):
                        kept[i].wait(e, n, FIRST_CH[4 * g + 4] // 2)
                    if g == 0:
                        dve.wait(e, n - 1, "t1")
                    if not (isinstance(n, int) and n == 0 and g == 0):
                        olo.wait(e, n, g)
                KT = 2 * g + 2
                for kt in range(PART * part, min(PART * (part + 1), KT)):
                    a = P if kt == KT - 1 else 0
                    for h in range(2):
                        hs = slice(h * HDIM, (h + 1) * HDIM)
                        ins = e.matmul(O[hs, a:GQ], vv[q][:, kt, hs], pT[h][g % 2][:, kt, a:GQ],
                                       start=(kt == 0), stop=(kt == KT - 1))
                if part == PARTS[g] - 1:
                    ins.then_inc(pv.sem, 1)

            for name in BEFORE:
                work(-1, 1, name)

            def behind(n, q, s):
                n_, q_, s_ = lagged(n, q, s)
                if exists(n_):
                    turn_p(n_, q_, s_)

            def group(n, q, s):
                g = group_at(n, q, s)
                if g and exists(g[0]):
                    values(*g)

            def unit(n, q, j, early, first, last):
                for s in range(STEPS):
                    scores(n, q, s, first)
                    behind(n, q, s)
                    for name in pieces(n):
                        if STEP_OF[name] == s:
                            work(n, q, name)
                    group(n, q, s)

            units(e, unit)
            for s in range(LAG + GROUPS):
                behind(UNITS, 0, s)
                group(UNITS, 0, s)
            for name in TAIL:
                work(UNITS, 0, name)

        def keep(e, n, s, parity):
            i, h = s // 2, s % 2
            g = i // 2
            for x, blocks in enumerate(CH[s]):
                ch = FIRST_CH[s] + x
                if ch % 2 != parity:
                    continue
                if s % 4 < 2 and not (isinstance(n, int) and n == 0 and g < 2):
                    pv.wait(e, n, g - 1)
                turned.wait(e, n, ch + 1)
                dst = pT[h][g % 2][:, x * HT:x * HT + blocks, (i % 2) * P:(i % 2 + 1) * P]
                src = T[ch % 2][:, 0:blocks * P].rearrange("p (b c) -> p b c", c=P)
                ins = e.activation(dst, src, ACT.Copy) if parity == 0 else e.tensor_copy(dst, src)
                ins.then_inc(kept[parity].sem, 1)

        @block.scalar
        def _(e):
            def softmax(n, q, s, first):
                i = s % RING
                m, t = (n, s - RING) if s >= RING else (n - 1, s - RING + STEPS)
                if real(m):
                    turned.wait(e, m, FIRST_CH[t + 1])
                negmax.wait(e, n, s + 1)
                off, w = shift(s), width(s)
                e.activation(pr[i][:, 0:w], S[s % 2][:, off:off + w], ACT.Exp, bias=negm[:, i:i + 1],
                             accum_out=rsum[:, i:i + 1]).then_inc(expd.sem, 1)

            def work(n, q, name):
                filled.wait(e, n, name)
                W = work_bank(name)
                if name == "xn":
                    apart(e, s_apart["act"])
                    ins = e.activation(xnh[:, bass.ds((n + AHEAD) % (2 * QT), 1), :, :].rearrange("p t m c -> p (t m c)"),
                                       W[:, 0:MODEL], ACT.Copy)
                elif name[0] == "v":
                    ins = e.activation(vT[:], W, ACT.Copy)
                else:
                    cols = slice(int(name[1]) * HALF, (int(name[1]) + 1) * HALF)
                    dst, scale = (qh, QSCALE) if name[0] == "q" else (kk, 1.0)
                    for h in range(2):
                        hs = slice(h * HDIM, (h + 1) * HDIM)
                        ins = e.activation(dst[1 - q][h][hs, cols], W[hs, :], ACT.Copy, scale=scale)
                ins.then_inc(act.sem, 1)

            for name in BEFORE:
                if name in BY_ACT:
                    work(-1, 1, name)

            def behind(n, q, s):
                n_, q_, s_ = lagged(n, q, s)
                if exists(n_):
                    keep(e, n_, s_, 0)

            def group(n, q, s):
                g = group_at(n, q, s)
                if g and exists(g[0]) and g[3] == PARTS[g[2]] - 1:
                    m, p_, g_, _ = g
                    pv.wait(e, m, g_ + 1)
                    e.activation(oh[p_][:, g_ * GQ:(g_ + 1) * GQ], O[:], ACT.Copy).then_inc(ohi.sem, 1)

            def unit(n, q, j, early, first, last):
                for s in range(STEPS):
                    behind(n, q, s)
                    softmax(n, q, s, first)
                    for name in pieces(n):
                        if STEP_OF[name] == s and name in BY_ACT:
                            work(n, q, name)
                    group(n, q, s)

            units(e, unit)
            for s in range(LAG + GROUPS):
                behind(UNITS, 0, s)
                group(UNITS, 0, s)

        @block.vector
        def _(e):
            def reciprocal(n, s):
                i = s % RING
                expd.wait(e, n, s + 1)
                e.reciprocal(rinv[:, i:i + 1], rsum[:, i:i + 1]).then_inc(recip.sem, 1)

            def work(n, q, name):
                if name in BY_ACT:
                    act.wait(e, n, name)
                else:
                    filled.wait(e, n, name)
                W = work_bank(name)
                if name == "xn":
                    slot = bass.ds((n + AHEAD) % (2 * QT), 1)
                    ins = e.tensor_tensor(xnl[:, slot, :, :].rearrange("p t m c -> p (t m c)"), W[:, 0:MODEL],
                                          xnh[:, slot, :, :].rearrange("p t m c -> p (t m c)").bitcast(F32), ALU.subtract)
                elif name[0] == "t":
                    f = int(name[1])
                    ins = e.tensor_copy(flat(vv[1 - q][:, f * HT:(f + 1) * HT, :]), W)
                elif name[0] == "o":
                    if name == "o0" and real(n - 1 if isinstance(n, int) else n):
                        wait_for_res(n)
                    at = ((n - 1) // PAIRS) % 2 * QT + 2 * int(name[1])
                    r = flat(res[:, bass.ds(at, 2), :])
                    ins = e.tensor_tensor(r, W, r, ALU.add)
                else:
                    cols = slice(int(name[1]) * HALF, (int(name[1]) + 1) * HALF)
                    for h in range(2):
                        hs, other = slice(h * HDIM, (h + 1) * HDIM), slice((1 - h) * HDIM, (2 - h) * HDIM)
                        if name[0] == "q":
                            ins = e.scalar_tensor_tensor(ql[1 - q][h][hs, cols], W[hs, :], QSCALE,
                                                         qh[1 - q][h][hs, cols].bitcast(F32), ALU.mult, ALU.subtract)
                        else:
                            ins = e.tensor_tensor(kk[1 - q][h][other, cols], W[hs, :],
                                                  kk[1 - q][h][hs, cols].bitcast(F32), ALU.subtract)
                ins.then_inc(dve.sem, 1)

            def wait_for_res(n):
                if isinstance(n, int):
                    if n >= 2:
                        rload.wait(e, min(n - 2, UNITS - 2 - 1), 16)
                else:
                    rload.wait(e, n - 2, 16)

            for name in BEFORE:
                if name in BY_DVE:
                    work(-1, 1, name)

            def behind(n, q, s):
                n_, q_, s_ = lagged(n, q, s)
                if exists(n_):
                    keep(e, n_, s_, 1)

            def group(n, q, s):
                g = group_at(n, q, s)
                if g and exists(g[0]) and g[3] == PARTS[g[2]] - 1:
                    m, p_, g_, _ = g
                    ohi.wait(e, m, g_ + 1)
                    cols = slice(g_ * GQ, (g_ + 1) * GQ)
                    e.tensor_tensor(ol[p_][:, cols], O[:], oh[p_][:, cols].bitcast(F32), ALU.subtract).then_inc(olo.sem, 1)

            def unit(n, q, j, early, first, last):
                for s in range(STEPS):
                    i = s % RING
                    score.wait(e, n, s + 1)
                    off, w = shift(s), width(s)
                    e.tensor_reduce(negm[:, i:i + 1], S[s % 2][:, off:off + w], AX.X, ALU.max,
                                    negate=True).then_inc(negmax.sem, 1)
                    if s:
                        reciprocal(n, s - 1)
                    elif not first:
                        reciprocal(n - 1, STEPS - 1)
                    behind(n, q, s)
                    for name in pieces(n):
                        if STEP_OF[name] == s and name in BY_DVE:
                            work(n, q, name)
                    group(n, q, s)

            units(e, unit)
            reciprocal(UNITS - 1, STEPS - 1)
            e.wait_ge(s_last_y, 16 * QT * TOPK)
            sums = [(t, j) for j in range(TOPK) for t in range(QT)]
            per = -(-len(sums) // (LAG + GROUPS))
            for s in range(LAG + GROUPS):
                behind(UNITS, 0, s)
                group(UNITS, 0, s)
                for t, j in sums[s * per:(s + 1) * per]:
                    if j and t == 0:
                        e.wait_ge(s_last_sum, 1)
                    r = res[:, (LAST + t) % (2 * QT), :]
                    ins = e.scalar_tensor_tensor(r, last_y[j][t], pick[:, LAST + t, TOPK + j:TOPK + j + 1].bitcast(F32), r,
                                                 ALU.mult, ALU.add)
                    if t == QT - 1:
                        ins.then_inc(s_last_sum, 1)
            e.wait_ge(s_last_sum, 2)
            for name in TAIL:
                work(UNITS, 0, name)

        @block.gpsimd
        def _(e):
            def split(n):
                filled.wait(e, n, "v1")
                apart(e, s_apart["pool"])
                wload.wait(e, n + 1, 16)
                apart(e, s_apart["pool"])
                split_weights(e, whi.sem, lambda: whi.wait(e, n + 1, 1), wlo.sem)

            def choose(m):
                summed.wait(e, m - 1, 1)
                e.tensor_copy(sel[:], pick[:, bass.ds(m, 1), :].rearrange("p t c -> p (t c)")).then_inc(picked.sem, 1)

            def fetch(m, j):
                picked.wait(e, m, 1)
                apart(e, s_apart["pool"])
                e.indirect_dma_start(yg[j][:], None, y_dram,
                                     bass.IndirectOffsetOnAxis(ap=sel[:, j:j + 1], axis=0)).then_inc(ygot.sem, 16)

            def weigh(m):
                ygot.wait(e, m, 32)
                apart(e, s_apart["pool"])
                for j in range(TOPK):
                    ins = e.tensor_scalar(yg[j][:], yg[j][:], sel[:, 2 + j:3 + j].bitcast(F32), 1.0, ALU.mult, ALU.mult)
                ins.then_inc(sum1.sem, 1)

            def add(m):
                sum1.wait(e, m, 1)
                e.tensor_tensor(yg[0][:], yg[0][:], yg[1][:], ALU.add).then_inc(sum2.sem, 1)

            def total(n, q):
                m = n - QT
                sum2.wait(e, m, 1)
                apart(e, s_apart["pool"])
                stored[q].wait(e, (m - q) // 2 - 1, 16)
                apart(e, s_apart["pool"])
                dve.wait(e, n if not isinstance(n, int) else min(n, UNITS), "o3")
                e.tensor_tensor(ot[q][:], flat(res[:, bass.ds(m % (2 * QT), 1), :]), yg[0][:], ALU.add).then_inc(summed.sem, 1)

            e.sem_inc(summed.sem, 1)
            split(-1)

            def unit(n, q, j, early, first, last):
                for s in range(STEPS):
                    i = s % RING
                    recip.wait(e, n, s + 1)
                    apart(e, s_apart["pool"])
                    e.tensor_scalar(pr[i][:, 0:width(s)], pr[i][:, 0:width(s)], rinv[:, i:i + 1], 1.0,
                                    ALU.mult, ALU.mult).then_inc(scaled.sem, 1)
                    if s == STEP_OF["v1"] + 1 and not (isinstance(n, int) and n > 1):
                        split(n)
                    if not early:
                        if s == 0:
                            choose(n - QT)
                        elif s in (1, 3):
                            fetch(n - QT, s // 2)
                        elif s == 5:
                            weigh(n - QT)
                        elif s == 6:
                            add(n - QT)
                        elif s == max(14, STEP_OF["o3"]):
                            total(n, q)
                    if last:
                        if s == 0:
                            score.wait(e, n - 1, STEPS)
                        t, j = s // TOPK, s % TOPK
                        e.indirect_dma_start(last_y[j][t], None, y_dram,
                                             bass.IndirectOffsetOnAxis(ap=pick[:, LAST + t, j:j + 1], axis=0)).then_inc(s_last_y, 16)

            units(e, unit)


def program(nc, x, w_qkv, w_out, wg, w1, b1, w2, b2, out):
    xn_dram = nc.dram_tensor("xn", (TOKENS, MODEL), F32).ap()
    y_dram = nc.dram_tensor("y", (SLOTS, MODEL), F32).ap()
    with ExitStack() as c:
        k = constants(nc, c)
        pick = c.enter_context(nc.sbuf_tensor("pick", [P, TILES, 4], U32))
        with ExitStack() as c1:
            slot_token = c1.enter_context(nc.sbuf_tensor("slot_token", [P, SLOTS // P], U32))
            raw, first_weights = weight_loads(nc, c1, w1, b1, w2)
            with ExitStack() as c2:
                logits = c2.enter_context(nc.sbuf_tensor("logits", [P, TILES, EXPERTS], F32))
                layernorm_and_router(nc, k, x, wg, xn_dram, logits)
                route(nc, k, logits, pick, slot_token, first_weights)
            experts(nc, k, xn_dram, slot_token, raw, w1, w2, b2, y_dram)
        attention_and_sum(nc, k, x, xn_dram, w_qkv, w_out, pick, y_dram, out)


_INS = ["L0_attn_x", "L0_attn_w_qkv", "L0_attn_w_out", "L0_ffn_wg", "L0_ffn_w1", "L0_ffn_b1", "L0_ffn_w2", "L0_ffn_b2"]


def kernel(**inputs):
    import concourse.bacc as bacc
    from concourse.bass_utils import run_bass_kernel_spmd

    nc = bacc.Bacc("TRN2", target_bir_lowering=False, num_devices=1)
    arrays, args = {}, []
    for name in _INS:
        a = np.ascontiguousarray(inputs[name])
        arrays[f"in_{name}"] = a
        args.append(nc.dram_tensor(f"in_{name}", a.shape, mybir.dt.from_np(a.dtype), kind="ExternalInput").ap())
    out = nc.dram_tensor("out", (BATCH, SEQ, MODEL), F32, kind="ExternalOutput").ap()
    program(nc, *args, out)
    r = run_bass_kernel_spmd(nc, [arrays], core_ids=[0])
    return r.results[0]["out"]
```
